# Optimizing a Trainium2 kernel written in Bass

```python
import numpy as np
import jax
import jax.numpy as jnp

def _softmax(x, axis=-1):
    return jax.nn.softmax(x, axis=axis)

def _gelu(x):
    return jax.nn.gelu(x, approximate=True)

def _silu(x):
    return jax.nn.silu(x)

def _sigmoid(x):
    return jax.nn.sigmoid(x)

def _layernorm(x, axis=-1, eps=1e-05):
    m = jnp.mean(x, axis=axis, keepdims=True)
    v = jnp.var(x, axis=axis, keepdims=True)
    return (x - m) / jnp.sqrt(v + eps)

def _scatter_add(tgt, idx, src, axis=0):
    return tgt.at[idx].add(src)

def _segment_sum(src, seg, n):
    return jax.ops.segment_sum(src, seg, n)
kernel_name = 'mk_xattn_ffn_d1_seqx_r8_ed7b4d'

def setup_inputs(seed: int=0):
    np.random.seed(seed)
    _w = jnp.asarray

    def _rec_inputs():
        import jax
        import jax.numpy as jnp
        _rk = jax.random.key(seed)
        x = -0.0002928 + 1 * jax.random.normal(jax.random.fold_in(_rk, 1), (2, 512, 128), jnp.float32)
        _lenS = 512 - jax.random.randint(jax.random.fold_in(_rk, 7), (2,), 0, max(1, 512 // 4) + 1, jnp.int32)
        _lenS2 = 32 - jax.random.randint(jax.random.fold_in(_rk, 8), (2,), 0, max(1, 32 // 4) + 1, jnp.int32)
        _ctx_1024P = jax.random.normal(jax.random.fold_in(_rk, 11), (2, 16, 128), jnp.float32)
        _ctx_1024c = jax.random.dirichlet(jax.random.fold_in(_rk, 511), 0.3 * jnp.ones((16,), jnp.float32), (2, 32))
        _ctx_1024t = jnp.einsum('bsk,bkd->bsd', _ctx_1024c, _ctx_1024P)
        _ctx_1024t = _ctx_1024t * jax.lax.rsqrt(jnp.mean(jnp.square(_ctx_1024t)) + 1e-12) * 0.953939
        ctx_1024 = -1.39393e-06 + 0.999914 * (_ctx_1024t + 0.3 * jax.random.normal(jax.random.fold_in(_rk, 611), (2, 32, 128), jnp.float32))
        return (x, ctx_1024)
    x, ctx_1024 = _rec_inputs()

    def _L0_xattn_setup():
        import jax, jax.numpy as jnp
        import numpy as np
        N_HEADS = 16
        HIDDEN = 128
        HEAD = HIDDEN // N_HEADS
        key = jax.random.key(seed)
        ks = jax.random.split(key, 11)
        B, S, H = (2, 256, HIDDEN)
        s = 1.0 / np.sqrt(H)
        return {'query': jax.random.normal(ks[0], (B, S, H), jnp.float32), 'key': jax.random.normal(ks[1], (B, S, H), jnp.float32), 'value': jax.random.normal(ks[2], (B, S, H), jnp.float32), 'Wq': jax.random.normal(ks[3], (H, H), jnp.float32) * s, 'bq': jnp.zeros((H,), jnp.float32), 'Wk': jax.random.normal(ks[4], (H, H), jnp.float32) * s, 'bk': jnp.zeros((H,), jnp.float32), 'Wv': jax.random.normal(ks[5], (H, H), jnp.float32) * s, 'bv': jnp.zeros((H,), jnp.float32), 'Wo': jax.random.normal(ks[6], (H, H), jnp.float32) * s, 'bo': jnp.zeros((H,), jnp.float32)}
    _L0_xattn_all = _L0_xattn_setup()
    _L0_xattn_in = {k: v for k, v in _L0_xattn_all.items() if k in ('Wq', 'bq', 'Wk', 'bk', 'Wv', 'bv', 'Wo', 'bo')}
    del _L0_xattn_all

    def _L0_ffn_setup():
        import jax, jax.numpy as jnp
        import numpy as np
        H = 128
        I = 64
        E = 32
        TOP_K = 6
        N_GROUP = 8
        TOPK_GROUP = 4
        SCALE = 2.5
        N_SHARED = 2
        SI = I * N_SHARED
        B, S = (2, 128)
        key = jax.random.key(seed)
        ks = jax.random.split(key, 8)
        x = jax.random.normal(ks[0], (B, S, H), jnp.float32)
        gate_weight = jax.random.normal(ks[1], (E, H), jnp.float32) * 0.02
        e_score_correction_bias = jax.random.normal(ks[2], (E,), jnp.float32) * 0.01
        experts_gate_up = jax.random.normal(ks[3], (E, 2 * I, H), jnp.float32) * 0.02
        experts_down = jax.random.normal(ks[4], (E, H, I), jnp.float32) * 0.02
        shared_gate_w = jax.random.normal(ks[5], (SI, H), jnp.float32) * 0.02
        shared_up_w = jax.random.normal(ks[6], (SI, H), jnp.float32) * 0.02
        shared_down_w = jax.random.normal(ks[7], (H, SI), jnp.float32) * 0.02
        return {'x': x, 'gate_weight': gate_weight, 'e_score_correction_bias': e_score_correction_bias, 'experts_gate_up': experts_gate_up, 'experts_down': experts_down, 'shared_gate_w': shared_gate_w, 'shared_up_w': shared_up_w, 'shared_down_w': shared_down_w}
    _L0_ffn_all = _L0_ffn_setup()
    _L0_ffn_in = {k: v for k, v in _L0_ffn_all.items() if k in ('gate_weight', 'e_score_correction_bias', 'experts_gate_up', 'experts_down', 'shared_gate_w', 'shared_up_w', 'shared_down_w')}
    del _L0_ffn_all
    return {'x': x, 'ctx_1024': ctx_1024, 'L0_xattn_Wq': _L0_xattn_in['Wq'], 'L0_xattn_bq': _L0_xattn_in['bq'], 'L0_xattn_Wk': _L0_xattn_in['Wk'], 'L0_xattn_bk': _L0_xattn_in['bk'], 'L0_xattn_Wv': _L0_xattn_in['Wv'], 'L0_xattn_bv': _L0_xattn_in['bv'], 'L0_xattn_Wo': _L0_xattn_in['Wo'], 'L0_xattn_bo': _L0_xattn_in['bo'], 'L0_ffn_gate_weight': _L0_ffn_in['gate_weight'], 'L0_ffn_e_score_correction_bias': _L0_ffn_in['e_score_correction_bias'], 'L0_ffn_experts_gate_up': _L0_ffn_in['experts_gate_up'], 'L0_ffn_experts_down': _L0_ffn_in['experts_down'], 'L0_ffn_shared_gate_w': _L0_ffn_in['shared_gate_w'], 'L0_ffn_shared_up_w': _L0_ffn_in['shared_up_w'], 'L0_ffn_shared_down_w': _L0_ffn_in['shared_down_w']}

def reference(x, ctx_1024, L0_xattn_Wq, L0_xattn_bq, L0_xattn_Wk, L0_xattn_bk, L0_xattn_Wv, L0_xattn_bv, L0_xattn_Wo, L0_xattn_bo, L0_ffn_gate_weight, L0_ffn_e_score_correction_bias, L0_ffn_experts_gate_up, L0_ffn_experts_down, L0_ffn_shared_gate_w, L0_ffn_shared_up_w, L0_ffn_shared_down_w):
    import jax
    import jax.numpy as jnp

    def _L0_xattn_ref(query, key, value, Wq, bq, Wk, bk, Wv, bv, Wo, bo):
        import jax, jax.numpy as jnp
        import numpy as np
        N_HEADS = 16
        HIDDEN = 128
        HEAD = HIDDEN // N_HEADS
        B, Sq, H = query.shape
        Sk = key.shape[1]
        q = (query @ Wq + bq).reshape(B, Sq, N_HEADS, HEAD).transpose(0, 2, 1, 3)
        k = (key @ Wk + bk).reshape(B, Sk, N_HEADS, HEAD).transpose(0, 2, 1, 3)
        v = (value @ Wv + bv).reshape(B, Sk, N_HEADS, HEAD).transpose(0, 2, 1, 3)
        scores = jnp.einsum('bhqd,bhkd->bhqk', q, k) / np.sqrt(HEAD).astype(np.float32)
        attn = jax.nn.softmax(scores, axis=-1)
        out = jnp.einsum('bhqk,bhkd->bhqd', attn, v)
        out = out.transpose(0, 2, 1, 3).reshape(B, Sq, H)
        return out @ Wo + bo

    def _L0_ffn_ref(x, gate_weight, e_score_correction_bias, experts_gate_up, experts_down, shared_gate_w, shared_up_w, shared_down_w):
        import jax, jax.numpy as jnp
        import numpy as np
        H = 128
        I = 64
        E = 32
        TOP_K = 6
        N_GROUP = 8
        TOPK_GROUP = 4
        SCALE = 2.5
        N_SHARED = 2
        SI = I * N_SHARED
        B, S = (2, 128)
        b, s, h = x.shape
        xf = x.reshape(-1, h)
        T = xf.shape[0]
        logits = xf.astype(jnp.float32) @ gate_weight.astype(jnp.float32).T
        scores = jax.nn.sigmoid(logits)
        sfc = scores + e_score_correction_bias[None, :]
        gs = E // N_GROUP
        group_scores = sfc.reshape(T, N_GROUP, gs).max(axis=-1)
        _, gidx = jax.lax.top_k(group_scores, TOPK_GROUP)
        gmask = jnp.zeros((T, N_GROUP), bool).at[jnp.arange(T)[:, None], gidx].set(True)
        smask = jnp.repeat(gmask, gs, axis=1)
        masked = jnp.where(smask, sfc, 0.0)
        _, topk_idx = jax.lax.top_k(masked, TOP_K)
        tw = jnp.take_along_axis(scores, topk_idx, axis=1)
        tw = tw / (tw.sum(-1, keepdims=True) + 1e-20)
        tw = (tw * SCALE).astype(xf.dtype)
        combine = jnp.zeros((T, E), xf.dtype).at[jnp.arange(T)[:, None], topk_idx].add(tw)

        def expert_step(acc, inp):
            gu, dn, c = inp
            g = xf @ gu[:I].T
            u = xf @ gu[I:].T
            o = jax.nn.silu(g) * u @ dn.T
            return (acc + c[:, None] * o, None)
        routed, _ = jax.lax.scan(expert_step, jnp.zeros_like(xf), (experts_gate_up, experts_down, combine.T))
        sh = jax.nn.silu(xf @ shared_gate_w.T) * (xf @ shared_up_w.T)
        shared_out = sh @ shared_down_w.T
        return (routed + shared_out).reshape(b, s, h)
    x = x + _L0_xattn_ref(_layernorm(x, axis=-1), ctx_1024, ctx_1024, L0_xattn_Wq, L0_xattn_bq, L0_xattn_Wk, L0_xattn_bk, L0_xattn_Wv, L0_xattn_bv, L0_xattn_Wo, L0_xattn_bo)
    x = x + _L0_ffn_ref(_layernorm(x, axis=-1), L0_ffn_gate_weight, L0_ffn_e_score_correction_bias, L0_ffn_experts_gate_up, L0_ffn_experts_down, L0_ffn_shared_gate_w, L0_ffn_shared_up_w, L0_ffn_shared_down_w)
    return x

_drawn_inputs = setup_inputs


def setup_inputs(seed=0):
    import zlib

    import numpy as np

    out = dict(_drawn_inputs(seed))
    spreads = {'L0_xattn_bq': (0.0, 0.299),
     'L0_xattn_bk': (0.0, 0.8),
     'L0_xattn_bv': (0.0, 0.1),
     'L0_xattn_bo': (0.0, 0.1)}
    factors = {'L0_ffn_gate_weight': 8.0,
     'L0_ffn_e_score_correction_bias': 8.0,
     'L0_ffn_experts_gate_up': 8.0,
     'L0_ffn_experts_down': 8.0,
     'L0_ffn_shared_gate_w': 8.0,
     'L0_ffn_shared_up_w': 8.0,
     'L0_ffn_shared_down_w': 8.0}
    for name, (base, spread) in spreads.items():
        noise = np.random.default_rng([zlib.crc32(name.encode()), seed]).standard_normal(out[name].shape)
        drawn = base * np.exp(spread * noise) if base else spread * noise
        out[name] = jnp.asarray(drawn.astype(out[name].dtype))
    for name, factor in factors.items():
        out[name] = (out[name] * factor).astype(out[name].dtype)
    return out
```

```python
from contextlib import ExitStack

import concourse.bass as bass
from concourse import mybir

F32 = mybir.dt.float32
F32R = mybir.dt.float32r
BF16 = mybir.dt.bfloat16
ALU = mybir.AluOpType
ACT = mybir.ActivationFunctionType
AXIS_X = mybir.AxisListType.X

P = 128
B = 2
SEQ = 512
TPB = SEQ // P
T = B * SEQ
HEADS, HD, KEYS = 16, 8, 32
HPG = P // KEYS
HG = HEADS // HPG
VE_W = HPG * HD + HPG
EXPERTS, GROUPS, TOP_GROUPS, TOP_K = 32, 8, 4, 6
EPG = EXPERTS // GROUPS
ROUTE_SCALE = 2.5
INTER = 64
PAIRS = EXPERTS // 2
W_GU, W_D = 2 * P, P
W_PAIR = W_GU + W_D
LOOPS = (PAIRS - 2) // 2
PARTS = 3
W_CUTS = [0, 3, 8, 13, PAIRS + 1]
EPS = 1e-5
SENTINEL = -3.0e38
TAKEN = 3.0e38

SMALL = [("ctx4T", B * P), ("wk", P), ("wv", P), ("wq", P), ("wo", P), ("bq", 1), ("bk", 1),
         ("bv", P), ("bo", P), ("gate", EXPERTS), ("ebias", EXPERTS)]


def columns(names):
    at, where = 0, {}
    for name, n in names:
        where[name] = (at, at + n)
        at += n
    return where, at


SMALL_AT, SMALL_W = columns(SMALL)


def xattn_moe(nc, x_tok, small_in, weights_in, out_t):
    ctx = ExitStack()
    with ctx:
        def sb(name, shape, dt=F32):
            return ctx.enter_context(nc.sbuf_tensor(name, shape, dt))

        def sem(name):
            return ctx.enter_context(nc.semaphore(name))

        x = sb("x", [P, T])
        small = sb("small", [P, SMALL_W])
        raw_w = sb("raw_w", [P, (PAIRS + 1) * W_PAIR])

        def part(name):
            return small[:, SMALL_AT[name][0]:SMALL_AT[name][1]]

        ident = sb("ident", [P, P])
        ident_bf = sb("ident_bf", [P, P], BF16)
        head_of_row = sb("head_of_row", [P, HEADS])
        local_head = sb("local_head", [P, HPG, HD])
        neg_pick = sb("neg_pick", [HEADS, HG, P])
        neg_pick_r = sb("neg_pick_r", [HEADS, HG, P], F32R)
        pick = sb("pick", [PARTS * EXPERTS, PAIRS * P], BF16)

        k_t = sb("k_t", [P, B * KEYS])
        k_hi = sb("k_hi", [P, B * KEYS], F32R)
        k_lo = sb("k_lo", [P, B * KEYS])
        kblk_hi = sb("kblk_hi", [P, B, HEADS, KEYS], F32R)
        kblk_lo = sb("kblk_lo", [P, B, HEADS, KEYS], F32R)
        v_rep = sb("v_rep", [P, B, P])
        v_ext = sb("v_ext", [P, B, HG, VE_W])
        wq_hi = sb("wq_hi", [P, P], F32R)
        wq_lo = sb("wq_lo", [P, P], F32R)
        stats = sb("stats", [P, B * TPB, 6])
        mv = sb("mv", [P, B * TPB, 2])
        var_e = sb("var_e", [P, B * TPB])
        rs_a = sb("rs_a", [P, B * TPB])
        rs_b = sb("rs_b", [P, B * TPB])
        rs_c = sb("rs_c", [P, B * TPB])
        rstd = sb("rstd", [P, B * TPB])
        xn = sb("xn", [P, T])
        xb = sb("xb", [P, T])
        xn_hi = sb("xn_hi", [P, T], F32R)
        xn_lo = sb("xn_lo", [P, T], F32R)
        q_hi = sb("q_hi", [P, T], F32R)
        q_lo = sb("q_lo", [P, T], F32R)
        smax = sb("smax", [P, B * TPB, HEADS])
        smax_t = sb("smax_t", [HEADS, T], F32R)
        probs = sb("probs", [P, B, HG, SEQ])
        rden = sb("rden", [P, B * TPB, HG, HPG])
        att = sb("att", [P, T])
        att_t = sb("att_t", [P, T])
        y = sb("y", [P, T])

        stats2 = sb("stats2", [P, B * TPB, 6])
        mv2 = sb("mv2", [P, B * TPB, 2])
        rstd2 = sb("rstd2", [P, B * TPB])
        yn = sb("yn", [P, T])
        yn_hi = sb("yn_hi", [P, T], F32R)
        yn_lo = sb("yn_lo", [P, T], F32R)
        gate_hi = sb("gate_hi", [P, EXPERTS], F32R)
        gate_lo = sb("gate_lo", [P, EXPERTS], F32R)
        exp_l = sb("exp_l", [P, B, TPB, EXPERTS])
        exp_1 = sb("exp_1", [P, B, TPB, EXPERTS])
        score = sb("score", [P, B, TPB, EXPERTS])
        sfc = sb("sfc", [P, B, TPB, EXPERTS])
        g_pad = GROUPS + TOP_GROUPS
        e_pad = EXPERTS + 8 - TOP_K
        g_max = sb("g_max", [P, B, TPB, g_pad])
        g_top = sb("g_top", [P, B, TPB, 8])
        g_mark = sb("g_mark", [P, B, TPB, g_pad])
        g_sel = sb("g_sel", [P, B, TPB, GROUPS])
        masked = sb("masked", [P, B, TPB, e_pad])
        e_top = sb("e_top", [P, B, TPB, 8])
        e_mark = sb("e_mark", [P, B, TPB, e_pad])
        chosen = sb("chosen", [P, B, TPB, EXPERTS])
        ch_sum = sb("ch_sum", [P, B, TPB])
        ch_sc = sb("ch_sc", [P, B, TPB])
        ch_rec = sb("ch_rec", [P, B, TPB])
        comb = sb("comb", [P, B, TPB, EXPERTS])
        comb_r1 = sb("comb_r1", [P, B, TPB, EXPERTS])
        comb_r2 = sb("comb_r2", [P, B, TPB, EXPERTS])
        comb3 = sb("comb3", [P, B, TPB, PARTS, EXPERTS], BF16)
        comb_t = sb("comb_t", [PARTS * EXPERTS, T], BF16)

        w_hi = [sb(f"w_hi{s}", [P, W_PAIR], F32R) for s in range(2)]
        w_lo = [sb(f"w_lo{s}", [P, W_PAIR], F32R) for s in range(2)]
        act_g = [sb(f"act_g{b}", [P, SEQ]) for b in range(B)]
        gu = [sb(f"gu{b}", [P, SEQ]) for b in range(B)]
        h = [sb(f"h{b}", [P, SEQ]) for b in range(B)]
        h_hi = [sb(f"h_hi{b}", [P, SEQ], F32R) for b in range(B)]
        h_lo = [sb(f"h_lo{b}", [P, SEQ], F32R) for b in range(B)]
        result = sb("result", [P, T])

        bank = [ctx.enter_context(nc.psum_tensor(f"bank{i}", [P, SEQ], F32)) for i in range(8)]
        kv_ps = bank[6]

        x_in = [sem(f"x_in{b}") for b in range(B)]
        small_in_s = sem("small_in")
        w_in = [sem(f"w_in{n}") for n in range(len(W_CUTS) - 1)]
        out_done = sem("out_done")
        consts = sem("consts")
        pool_step = sem("pool_step")
        kblk_ready = sem("kblk_ready")
        vext_ready = sem("vext_ready")
        h_lo_ready = sem("h_lo_ready")
        act_step = sem("act_step")
        ln_exp = sem("ln_exp")
        xn_hi_ready = sem("xn_hi_ready")
        q_hi_ready = sem("q_hi_ready")
        probs_ready = sem("probs_ready")
        att_t_ready = sem("att_t_ready")
        yn_hi_ready = sem("yn_hi_ready")
        exp_l_ready = sem("exp_l_ready")
        comb_t_ready = sem("comb_t_ready")
        silu_ready = sem("silu_ready")
        h_hi_ready = sem("h_hi_ready")
        gu_hi_ready = sem("gu_hi_ready")
        d_hi_ready = sem("d_hi_ready")
        vec_step = sem("vec_step")
        kv_read = sem("kv_read")
        small_hi_ready = sem("small_hi_ready")
        var_ready = sem("var_ready")
        xn_ready = sem("xn_ready")
        xn_lo_ready = sem("xn_lo_ready")
        q_lo_ready = sem("q_lo_ready")
        smax_ready = sem("smax_ready")
        smax_t_ready = sem("smax_t_ready")
        att_ready = sem("att_ready")
        y_ready = sem("y_ready")
        yn_ready = sem("yn_ready")
        yn_lo_ready = sem("yn_lo_ready")
        comb3_ready = sem("comb3_ready")
        gu_ready = sem("gu_ready")
        h_ready = sem("h_ready")
        gu_lo_ready = sem("gu_lo_ready")
        d_lo_ready = sem("d_lo_ready")
        result_ready = [sem(f"result_ready{b}") for b in range(B)]
        kv_done = sem("kv_done")
        xn_t_done = sem("xn_t_done")
        q_done = sem("q_done")
        score_done = sem("score_done")
        smax_t_done = sem("smax_t_done")
        score_t_done = sem("score_t_done")
        av_done = sem("av_done")
        att_t_done = sem("att_t_done")
        proj_done = sem("proj_done")
        yn_t_done = sem("yn_t_done")
        logits_done = sem("logits_done")
        comb_t_done = sem("comb_t_done")
        gate_done = sem("gate_done")
        up_done = sem("up_done")
        spread_done = sem("spread_done")
        down_done = sem("down_done")

        def tile_of(tensor, b, t, w=P):
            i = b * TPB + t
            return tensor[:, i * w:(i + 1) * w]

        def row(tensor, b):
            return tensor[:, b * SEQ:(b + 1) * SEQ]

        block = ctx.enter_context(nc.Block())

        @block.sync
        def _(sp):
            for b in range(B):
                sp.dma_start(row(x, b), x_tok[:, b * SEQ:(b + 1) * SEQ]).then_inc(x_in[b], 16)
            for n, (lo, hi) in enumerate(zip(W_CUTS, W_CUTS[1:])):
                sp.dma_start(raw_w[:, lo * W_PAIR:hi * W_PAIR],
                             weights_in[:, lo * W_PAIR:hi * W_PAIR]).then_inc(w_in[n], 16)
            for b in range(B):
                sp.wait_ge(result_ready[b], 1)
                sp.dma_start(out_t[:, b * SEQ:(b + 1) * SEQ], row(result, b)).then_inc(out_done, 16)
            sp.wait_ge(out_done, 16 * B)

        @block.gpsimd
        def _(pool):
            steps = [0]

            def step(ins):
                steps[0] += 1
                ins.then_inc(pool_step, 1)
                pool.wait_ge(pool_step, steps[0])

            step(nc.gpsimd.memset(ident[:], 0.0))
            nc.gpsimd.affine_select(out=ident[:], in_=ident[:], compare_op=ALU.not_equal, fill=1.0, base=0,
                                    pattern=[[-1, P]], channel_multiplier=1).then_inc(consts, 1)
            step(nc.gpsimd.memset(head_of_row[:], 1.0))
            step(nc.gpsimd.affine_select(out=head_of_row[:], in_=head_of_row[:], compare_op=ALU.is_ge, fill=0.0,
                                         base=0, pattern=[[-HD, HEADS]], channel_multiplier=1))
            step(nc.gpsimd.affine_select(out=head_of_row[:], in_=head_of_row[:], compare_op=ALU.is_ge, fill=0.0,
                                         base=HD - 1, pattern=[[HD, HEADS]], channel_multiplier=-1))
            step(nc.gpsimd.memset(local_head[:], 1.0))
            step(nc.gpsimd.affine_select(out=local_head[:], in_=local_head[:], compare_op=ALU.is_ge, fill=0.0,
                                         base=0, pattern=[[-KEYS, HPG], [0, HD]], channel_multiplier=1))
            step(nc.gpsimd.affine_select(out=local_head[:], in_=local_head[:], compare_op=ALU.is_ge, fill=0.0,
                                         base=KEYS - 1, pattern=[[KEYS, HPG], [0, HD]], channel_multiplier=-1))
            pool.wait_ge(kv_read, 1)
            for b in range(B):
                for part_k, blk in ((k_hi[:].bitcast(F32), kblk_hi), (k_lo[:], kblk_lo)):
                    keys = part_k[:, b * KEYS:(b + 1) * KEYS].unsqueeze(1).broadcast_to([P, HEADS, KEYS])
                    heads = head_of_row[:].unsqueeze(2).broadcast_to([P, HEADS, KEYS])
                    nc.gpsimd.tensor_tensor(blk[:, b], keys, heads, ALU.mult).then_inc(kblk_ready, 1)
            pool.wait_ge(kv_read, 2)
            for b in range(B):
                mask = local_head[:].rearrange("p h d -> p (h d)").unsqueeze(1).broadcast_to([P, HG, HPG * HD])
                nc.gpsimd.tensor_tensor(v_ext[:, b, :, 0:HPG * HD],
                                        v_rep[:, b].rearrange("p (g c) -> p g c", g=HG), mask,
                                        ALU.mult).then_inc(vext_ready, 1)
                for g in range(HG):
                    nc.gpsimd.tensor_copy(v_ext[:, b, g, HPG * HD:VE_W],
                                          local_head[:, :, 0]).then_inc(vext_ready, 1)
            step(nc.gpsimd.memset(neg_pick[:], -1.0))
            step(nc.gpsimd.affine_select(out=neg_pick[:], in_=neg_pick[:].rearrange("p g (h k) -> p g h k", h=HPG),
                                         compare_op=ALU.is_equal, fill=0.0, base=0,
                                         pattern=[[-HPG, HG], [-1, HPG], [0, KEYS]], channel_multiplier=1))
            nc.gpsimd.tensor_copy(neg_pick_r[:], neg_pick[:]).then_inc(consts, 1)
            for b in range(B):
                pool.wait_ge(small_in_s, 16)
                pool.wait_ge(x_in[b], 16)
                nc.gpsimd.tensor_tensor(row(xb, b).rearrange("p (t f) -> p t f", t=TPB),
                                        row(x, b).rearrange("p (t f) -> p t f", t=TPB),
                                        part("bo").unsqueeze(1).broadcast_to([P, TPB, P]),
                                        ALU.add).then_inc(consts, 1)
            nc.gpsimd.tensor_copy(ident_bf[:], ident[:]).then_inc(consts, 1)
            step(nc.gpsimd.memset(pick[:], 0.0))
            for k in range(PARTS):
                step(nc.gpsimd.affine_select(out=pick[:], in_=pick[:], compare_op=ALU.not_equal, fill=1.0,
                                             base=-k * EXPERTS, pattern=[[-2, PAIRS], [-1, 2], [0, INTER]],
                                             channel_multiplier=1))
            step(nc.gpsimd.memset(g_max[:], SENTINEL))
            nc.gpsimd.memset(masked[:], SENTINEL).then_inc(consts, 1)

            def low_part(pair, b):
                pool.wait_ge(h_hi_ready, 2 * pair + b + 1)
                nc.gpsimd.tensor_tensor(h_lo[b][:], h[b][:], h_hi[b][:].bitcast(F32),
                                        ALU.subtract).then_inc(h_lo_ready, 1)

            low_part(0, 0)
            low_part(0, 1)
            with pool.Fori(0, PAIRS // 2) as it:
                for s in range(2):
                    for b in range(B):
                        low_part(it * 2 + (1 + s), b)

        @block.scalar
        def _(act):
            act.dma_start(small[:], small_in[:, :]).then_inc(small_in_s, 16)
            steps = [0]

            def step(ins):
                steps[0] += 1
                ins.then_inc(act_step, 1)
                act.wait_ge(act_step, steps[0])

            def inverse_root(n, b):
                v = slice(b * TPB, (b + 1) * TPB)
                act.wait_ge(var_ready, n)
                step(nc.scalar.activation(rs_b[:, v], var_e[:, v], ACT.Ln))
                nc.scalar.activation(rs_a[:, v], rs_b[:, v], ACT.Exp, scale=-0.5).then_inc(ln_exp, 1)

            for b in range(B):
                inverse_root(b + 1, b)
            for b in range(B):
                act.wait_ge(xn_t_done, b + 1)
                nc.scalar.activation(row(xn_hi, b), bank[b][:], ACT.Copy).then_inc(xn_hi_ready, 1)
            for b in range(B):
                act.wait_ge(q_done, b + 1)
                nc.scalar.activation(row(q_hi, b), bank[2 + b][:], ACT.Identity,
                                     bias=part("bq")).then_inc(q_hi_ready, 1)
            for b in range(B):
                for g in range(HG):
                    act.wait_ge(score_t_done, b * HG + g + 1)
                    nc.scalar.activation(probs[:, b, g], bank[4 + g][:], ACT.Exp).then_inc(probs_ready, 1)
            for b in range(B):
                act.wait_ge(att_t_done, b + 1)
                nc.scalar.activation(row(att_t, b), bank[2 + b][:], ACT.Copy).then_inc(att_t_ready, 1)
                inverse_root(B + b + 1, b)
            for b in range(B):
                act.wait_ge(yn_t_done, b + 1)
                nc.scalar.activation(row(yn_hi, b), bank[2 + b][:], ACT.Copy).then_inc(yn_hi_ready, 1)
                act.wait_ge(logits_done, b + 1)
                nc.scalar.activation(exp_l[:, b].rearrange("p t e -> p (t e)"), bank[6 + b][:, 0:TPB * EXPERTS],
                                     ACT.Exp, scale=-1.0).then_inc(exp_l_ready, 1)

            def silu(pair, b, first=False):
                act.wait_ge(gate_done, 2 * pair + b + 1)
                if not first:
                    act.wait_ge(gu_ready, 2 * pair + b - 1)
                nc.scalar.activation(act_g[b][:], bank[2 + b][:], ACT.Silu).then_inc(silu_ready, 1)

            def high_part(pair, b, first=False):
                act.wait_ge(h_ready, 2 * pair + b + 1)
                if not first:
                    act.wait_ge(down_done, 2 * pair + b - 1)
                nc.scalar.activation(h_hi[b][:], h[b][:], ACT.Copy).then_inc(h_hi_ready, 1)

            def weights_high(pair, slot, at, n, ready):
                nc.scalar.activation(w_hi[slot][:, at:at + n], raw_w[:, bass.ds(pair * W_PAIR + at, n)],
                                     ACT.Copy).then_inc(ready, 1)

            act.wait_ge(w_in[0], 16)
            weights_high(0, 0, 0, W_GU, gu_hi_ready)
            weights_high(0, 0, W_GU, W_D, d_hi_ready)
            weights_high(1, 1, 0, W_GU, gu_hi_ready)
            silu(0, 0, first=True)
            silu(0, 1, first=True)
            high_part(0, 0, first=True)
            for b in range(B):
                act.wait_ge(comb_t_done, b + 1)
                nc.scalar.activation(row(comb_t, b), bank[6 + b][:].bitcast(BF16)[0:PARTS * EXPERTS, SEQ:2 * SEQ],
                                     ACT.Copy).then_inc(comb_t_ready, 1)
            for arrived in w_in[1:]:
                act.wait_ge(arrived, 16)

            def pair_steps(pair, slot, last=False):
                if not last:
                    act.wait_ge(up_done, 2 * pair)
                    weights_high(pair + 1, 1 - slot, 0, W_GU, gu_hi_ready)
                silu(pair, 0)
                act.wait_ge(h_ready, 2 * pair)
                nc.scalar.activation(h_hi[1][:], h[1][:], ACT.Copy).then_inc(h_hi_ready, 1)
                silu(pair, 1)
                weights_high(pair, slot, W_GU, W_D, d_hi_ready)
                high_part(pair, 0)

            with act.Fori(0, LOOPS) as it:
                for s in range(2):
                    pair_steps(it * 2 + (1 + s), 1 - s)
            pair_steps(PAIRS - 1, 1)
            pair_steps(PAIRS, 0, last=True)
            high_part(PAIRS, 1)
            act.wait_ge(down_done, 2 * PAIRS + 1)
            nc.scalar.activation(row(result, 0), bank[0][:], ACT.Copy).then_inc(result_ready[0], 1)

        @block.vector
        def _(dve):
            steps = [0]

            def mark(ins):
                steps[0] += 1
                ins.then_inc(vec_step, 1)

            def settle():
                dve.wait_ge(vec_step, steps[0])

            def step(ins):
                mark(ins)
                settle()

            def moments(src, st, out, b):
                for t in range(TPB):
                    mark(nc.vector.bn_stats(st[:, b * TPB + t], tile_of(src, b, t)))
                settle()
                for t in range(TPB):
                    mark(nc.vector.bn_aggr(out[:, b * TPB + t], st[:, b * TPB + t]))
                settle()
                v = slice(b * TPB, (b + 1) * TPB)
                nc.vector.tensor_scalar(var_e[:, v], out[:, v, 1], EPS, None, ALU.add).then_inc(var_ready, 1)

            def normalise(src, m, r, out, b, n, ready):
                v = slice(b * TPB, (b + 1) * TPB)
                dve.wait_ge(ln_exp, n)
                step(nc.vector.tensor_tensor(rs_b[:, v], rs_a[:, v], rs_a[:, v], ALU.mult))
                step(nc.vector.scalar_tensor_tensor(rs_c[:, v], rs_b[:, v], -0.5, var_e[:, v], ALU.mult, ALU.mult))
                step(nc.vector.scalar_tensor_tensor(r[:, v], rs_c[:, v], 1.5, rs_a[:, v], ALU.add, ALU.mult))
                for t in range(TPB):
                    i = b * TPB + t
                    nc.vector.tensor_scalar(tile_of(out, b, t), tile_of(src, b, t), m[:, i, 0:1], r[:, i:i + 1],
                                            ALU.subtract, ALU.mult).then_inc(ready, 1)

            for b in range(B):
                dve.wait_ge(x_in[b], 16)
                moments(x, stats, mv, b)
                if b == 0:
                    dve.wait_ge(small_in_s, 16)
                    mark(nc.vector.tensor_copy(wq_hi[:], part("wq")))
                    mark(nc.vector.tensor_copy(gate_hi[:], part("gate")))
                    settle()
                    nc.vector.tensor_tensor(wq_lo[:], part("wq"), wq_hi[:].bitcast(F32),
                                            ALU.subtract).then_inc(small_hi_ready, 1)
                    nc.vector.tensor_tensor(gate_lo[:], part("gate"), gate_hi[:].bitcast(F32),
                                            ALU.subtract).then_inc(small_hi_ready, 1)
                    dve.wait_ge(kv_done, 1)
                    step(nc.vector.tensor_scalar(k_t[:], kv_ps[:, 0:B * KEYS], part("bk"), HD ** -0.5,
                                                 ALU.add, ALU.mult))
                    step(nc.vector.tensor_copy(k_hi[:], k_t[:]))
                    nc.vector.tensor_tensor(k_lo[:], k_t[:], k_hi[:].bitcast(F32), ALU.subtract).then_inc(kv_read, 1)
                    nc.vector.tensor_tensor(v_rep[:], kv_ps[:, P:P + B * P].rearrange("p (b f) -> p b f", b=B),
                                            part("bv").unsqueeze(1).broadcast_to([P, B, P]),
                                            ALU.add).then_inc(kv_read, 1)
                normalise(x, mv, rstd, xn, b, b + 1, xn_ready)
            for b in range(B):
                dve.wait_ge(xn_hi_ready, b + 1)
                nc.vector.tensor_tensor(row(xn_lo, b), bank[b][:], row(xn_hi, b).bitcast(F32),
                                        ALU.subtract).then_inc(xn_lo_ready, 1)
            for b in range(B):
                dve.wait_ge(q_hi_ready, b + 1)
                nc.vector.scalar_tensor_tensor(row(q_lo, b), bank[2 + b][:], part("bq"), row(q_hi, b).bitcast(F32),
                                               ALU.add, ALU.subtract).then_inc(q_lo_ready, 1)
            for b in range(B):
                for t in range(TPB):
                    i = b * TPB + t
                    dve.wait_ge(score_done, i + 1)
                    nc.vector.tensor_reduce(out=smax[:, i], in_=bank[4 + t][:].rearrange("p (h k) -> p h k", k=KEYS),
                                            op=ALU.max, axis=AXIS_X).then_inc(smax_ready, 1)
                dve.wait_ge(smax_t_done, b + 1)
                nc.vector.tensor_copy(row(smax_t, b), bank[b][0:HEADS, :]).then_inc(smax_t_ready, 1)
            for b in range(B):
                for half, where in ((0, bank[2 + b]), (1, bank[b])):
                    i = b * TPB + 2 * half
                    dve.wait_ge(av_done, b * 2 + half + 1)
                    sums = where[:, 0:2 * HG * VE_W].rearrange("p (g c) -> p g c", c=VE_W)
                    dens = rden[:, i:i + 2].rearrange("p t g h -> p (t g) h")
                    step(nc.vector.reciprocal(dens, sums[:, :, HPG * HD:VE_W]))
                    nc.vector.tensor_tensor(
                        att[:, i * P:(i + 2) * P].rearrange("p (g h d) -> p g h d", h=HPG, d=HD),
                        sums[:, :, 0:HPG * HD].rearrange("p g (h d) -> p g h d", d=HD),
                        dens.unsqueeze(3).broadcast_to([P, 2 * HG, HPG, HD]), ALU.mult).then_inc(att_ready, 1)
            for b in range(B):
                dve.wait_ge(proj_done, b + 1)
                dve.wait_ge(consts, 4)
                nc.vector.tensor_tensor(row(y, b), bank[b][:], row(xb, b), ALU.add).then_inc(y_ready, 1)
                dve.wait_ge(y_ready, b + 1)
                moments(y, stats2, mv2, b)
                normalise(y, mv2, rstd2, yn, b, B + b + 1, yn_ready)

            def low_yn(b):
                dve.wait_ge(yn_hi_ready, b + 1)
                nc.vector.tensor_tensor(row(yn_lo, b), bank[2 + b][:], row(yn_hi, b).bitcast(F32),
                                        ALU.subtract).then_inc(yn_lo_ready, 1)

            def route(b):
                flat = "p t e -> p (t e)"
                dve.wait_ge(exp_l_ready, b + 1)
                step(nc.vector.tensor_scalar(exp_1[:, b], exp_l[:, b], 1.0, None, ALU.add))
                step(nc.vector.reciprocal(score[:, b], exp_1[:, b]))
                step(nc.vector.tensor_tensor(sfc[:, b], score[:, b],
                                             part("ebias").unsqueeze(1).broadcast_to([P, TPB, EXPERTS]), ALU.add))
                step(nc.vector.tensor_reduce(out=g_max[:, b, :, 0:GROUPS],
                                             in_=sfc[:, b].rearrange("p t (g e) -> p t g e", e=EPG),
                                             op=ALU.max, axis=AXIS_X))
                for t in range(TPB):
                    mark(nc.vector.max(g_top[:, b, t], g_max[:, b, t, 0:GROUPS]))
                settle()
                step(nc.vector.memset(g_top[:, b, :, TOP_GROUPS:8], SENTINEL))
                for t in range(TPB):
                    mark(nc.vector.match_replace(out=g_mark[:, b, t], in_to_replace=g_top[:, b, t],
                                                 in_values=g_max[:, b, t], imm_value=TAKEN))
                settle()
                step(nc.vector.tensor_scalar(g_sel[:, b], g_mark[:, b, :, 0:GROUPS], TAKEN, None, ALU.is_equal))
                step(nc.vector.tensor_tensor(
                    masked[:, b, :, 0:EXPERTS].rearrange("p t (g e) -> p t g e", e=EPG),
                    sfc[:, b].rearrange("p t (g e) -> p t g e", e=EPG),
                    g_sel[:, b].unsqueeze(3).broadcast_to([P, TPB, GROUPS, EPG]), ALU.mult))
                for t in range(TPB):
                    mark(nc.vector.max(e_top[:, b, t], masked[:, b, t, 0:EXPERTS]))
                settle()
                step(nc.vector.memset(e_top[:, b, :, TOP_K:8], SENTINEL))
                for t in range(TPB):
                    mark(nc.vector.match_replace(out=e_mark[:, b, t], in_to_replace=e_top[:, b, t],
                                                 in_values=masked[:, b, t], imm_value=TAKEN))
                settle()
                step(nc.vector.scalar_tensor_tensor(chosen[:, b], e_mark[:, b, :, 0:EXPERTS], TAKEN, score[:, b],
                                                    ALU.is_equal, ALU.mult))
                step(nc.vector.tensor_reduce(out=ch_sum[:, b], in_=chosen[:, b], op=ALU.add, axis=AXIS_X))
                step(nc.vector.tensor_scalar(ch_sc[:, b], ch_sum[:, b], 1e-20, 1.0 / ROUTE_SCALE, ALU.add, ALU.mult))
                step(nc.vector.reciprocal(ch_rec[:, b], ch_sc[:, b]))
                step(nc.vector.tensor_tensor(comb[:, b], chosen[:, b],
                                             ch_rec[:, b].unsqueeze(2).broadcast_to([P, TPB, EXPERTS]), ALU.mult))
                step(nc.vector.tensor_copy(comb3[:, b, :, 0], comb[:, b]))
                step(nc.vector.tensor_tensor(comb_r1[:, b], comb[:, b], comb3[:, b, :, 0], ALU.subtract))
                step(nc.vector.tensor_copy(comb3[:, b, :, 1], comb_r1[:, b]))
                step(nc.vector.tensor_tensor(comb_r2[:, b], comb_r1[:, b], comb3[:, b, :, 1], ALU.subtract))
                nc.vector.tensor_copy(comb3[:, b, :, 2], comb_r2[:, b]).then_inc(comb3_ready, 1)

            def weights_low(pair, slot, at, n, ready, hi_ready):
                dve.wait_ge(hi_ready, pair + 1)
                nc.vector.tensor_tensor(w_lo[slot][:, at:at + n], raw_w[:, bass.ds(pair * W_PAIR + at, n)],
                                        w_hi[slot][:, at:at + n].bitcast(F32), ALU.subtract).then_inc(ready, 1)

            def gated(pair, b, first=False):
                dve.wait_ge(silu_ready, 2 * pair + b + 1)
                dve.wait_ge(up_done, 2 * pair + b + 1)
                if not first:
                    dve.wait_ge(h_ready, 2 * pair + b - 1)
                nc.vector.tensor_tensor(gu[b][:], bank[4 + b][:], act_g[b][:], ALU.mult).then_inc(gu_ready, 1)

            def weighted(pair, b):
                dve.wait_ge(spread_done, 2 * pair + b - 1)
                dve.wait_ge(gu_ready, 2 * pair + b + 1)
                dve.wait_ge(h_lo_ready, 2 * pair + b - 1)
                nc.vector.tensor_tensor(h[b][:], bank[6 + b][:], gu[b][:], ALU.mult).then_inc(h_ready, 1)

            low_yn(0)
            low_yn(1)
            dve.wait_ge(w_in[0], 16)
            weights_low(0, 0, 0, W_GU, gu_lo_ready, gu_hi_ready)
            weights_low(0, 0, W_GU, W_D, d_lo_ready, d_hi_ready)
            weights_low(1, 1, 0, W_GU, gu_lo_ready, gu_hi_ready)
            dve.wait_ge(consts, 6)
            for b in range(B):
                route(b)
            for b in range(B):
                gated(0, b, first=True)
                dve.wait_ge(gu_ready, b + 1)
                nc.vector.tensor_copy(h[b][:], gu[b][:]).then_inc(h_ready, 1)
            for arrived in w_in[1:]:
                dve.wait_ge(arrived, 16)

            def pair_steps(pair, slot, last=False):
                if not last:
                    weights_low(pair + 1, 1 - slot, 0, W_GU, gu_lo_ready, gu_hi_ready)
                gated(pair, 0)
                weighted(pair, 0)
                gated(pair, 1)
                weights_low(pair, slot, W_GU, W_D, d_lo_ready, d_hi_ready)
                weighted(pair, 1)

            with dve.Fori(0, LOOPS) as it:
                for s in range(2):
                    pair_steps(it * 2 + (1 + s), 1 - s)
            pair_steps(PAIRS - 1, 1)
            pair_steps(PAIRS, 0, last=True)
            dve.wait_ge(down_done, 2 * PAIRS + 2)
            nc.vector.tensor_copy(row(result, 1), bank[1][:]).then_inc(result_ready[1], 1)

        @block.tensor
        def _(pe):
            def wide(out, pairs, start=True, stop=True):
                for n, (lhs_t, rhs) in enumerate(pairs):
                    last = nc.tensor.matmul(out, lhs_t, rhs, start=start and n == 0,
                                            stop=stop and n == len(pairs) - 1)
                return last

            pe.wait_ge(small_in_s, 16)
            ctx_t = part("ctx4T").rearrange("p (b r k) -> p b r k", b=B, r=HPG)
            nc.tensor.matmul(kv_ps[:, 0:B * KEYS], part("wk"), ctx_t[:, :, 0, :], start=True, stop=True)
            for b in range(B):
                last = nc.tensor.matmul(kv_ps[:, P + b * P:P + (b + 1) * P], part("ctx4T")[:, b * P:(b + 1) * P],
                                        part("wv"), start=True, stop=True)
            last.then_inc(kv_done, 1)
            for b in range(B):
                for t in range(TPB):
                    pe.wait_ge(xn_ready, b * TPB + t + 1)
                    if b == 0 and t == 0:
                        pe.wait_ge(consts, 1)
                    last = nc.tensor.transpose(bank[b][:, t * P:(t + 1) * P], tile_of(xn, b, t), ident[:])
                last.then_inc(xn_t_done, 1)
            pe.wait_ge(small_hi_ready, 1)
            for b in range(B):
                pe.wait_ge(xn_hi_ready, b + 1)
                pe.wait_ge(xn_lo_ready, b + 1)
                wide(bank[2 + b][:], [(wq_hi[:], row(xn_hi, b)), (wq_hi[:], row(xn_lo, b)),
                                      (wq_lo[:], row(xn_hi, b))]).then_inc(q_done, 1)
            pe.wait_ge(kblk_ready, 4)
            pe.wait_ge(consts, 2)
            for b in range(B):
                for t in range(TPB):
                    if b == 0:
                        pe.wait_ge(q_hi_ready, 1)
                    else:
                        pe.wait_ge(q_hi_ready, 2)
                        pe.wait_ge(probs_ready, (b - 1) * HG + t + 1)
                    nc.tensor.matmul(bank[4 + t][:], tile_of(q_hi, b, t),
                                     kblk_hi[:, b].rearrange("p h k -> p (h k)"),
                                     start=True, stop=True).then_inc(score_done, 1)
                for t in range(TPB):
                    i = b * TPB + t
                    pe.wait_ge(smax_ready, i + 1)
                    if t == 0:
                        pe.wait_ge(xn_lo_ready, b + 1)
                    last = nc.tensor.transpose(bank[b][0:HEADS, t * P:(t + 1) * P], smax[:, i], ident[:])
                last.then_inc(smax_t_done, 1)
                pe.wait_ge(q_lo_ready, b + 1)
                pe.wait_ge(smax_t_ready, b + 1)
                for g in range(HG):
                    hs = slice(g * HPG, (g + 1) * HPG)
                    k_h = kblk_hi[:, b, hs].rearrange("p h k -> p (h k)")
                    k_l = kblk_lo[:, b, hs].rearrange("p h k -> p (h k)")
                    wide(bank[4 + g][:], [(k_h, row(q_hi, b)), (k_h, row(q_lo, b)), (k_l, row(q_hi, b)),
                                          (neg_pick_r[:, g], row(smax_t, b))]).then_inc(score_t_done, 1)
            pe.wait_ge(vext_ready, B * (1 + HG))
            for b in range(B):
                for half, where in ((0, bank[2 + b]), (1, bank[b])):
                    for t2 in range(2):
                        t = 2 * half + t2
                        for g in range(HG):
                            pe.wait_ge(probs_ready, b * HG + g + 1)
                            at = (t2 * HG + g) * VE_W
                            last = nc.tensor.matmul(where[:, at:at + VE_W], probs[:, b, g, t * P:(t + 1) * P],
                                                    v_ext[:, b, g], start=True, stop=True)
                    last.then_inc(av_done, 1)
            for b in range(B):
                pe.wait_ge(att_ready, 2 * b + 2)
                for t in range(TPB):
                    last = nc.tensor.transpose(bank[2 + b][:, t * P:(t + 1) * P], tile_of(att, b, t), ident[:])
                last.then_inc(att_t_done, 1)
            for b in range(B):
                pe.wait_ge(att_t_ready, b + 1)
                for t in range(TPB):
                    last = nc.tensor.matmul(bank[b][:, t * P:(t + 1) * P], tile_of(att_t, b, t), part("wo"),
                                            start=True, stop=True)
                last.then_inc(proj_done, 1)
            for b in range(B):
                for t in range(TPB):
                    pe.wait_ge(yn_ready, b * TPB + t + 1)
                    last = nc.tensor.transpose(bank[2 + b][:, t * P:(t + 1) * P], tile_of(yn, b, t), ident[:])
                last.then_inc(yn_t_done, 1)
            pe.wait_ge(small_hi_ready, 2)
            for b in range(B):
                pe.wait_ge(yn_hi_ready, b + 1)
                pe.wait_ge(yn_lo_ready, b + 1)
                for t in range(TPB):
                    out = bank[6 + b][:, t * EXPERTS:(t + 1) * EXPERTS]
                    last = wide(out, [(tile_of(yn_hi, b, t), gate_hi[:]), (tile_of(yn_hi, b, t), gate_lo[:]),
                                      (tile_of(yn_lo, b, t), gate_hi[:])])
                last.then_inc(logits_done, 1)

            def gate_up(pair, b, slot):
                g, u = slice(0, P), slice(P, W_GU)
                for where, w, done in ((bank[2 + b], g, gate_done), (bank[4 + b], u, up_done)):
                    if done is gate_done:
                        waits = silu_ready
                    else:
                        waits = gu_ready
                    if not (isinstance(pair, int) and pair == 0):
                        pe.wait_ge(waits, 2 * pair + b - 1)
                    wide(where[:], [(w_hi[slot][:, w], row(yn_hi, b)), (w_hi[slot][:, w], row(yn_lo, b)),
                                    (w_lo[slot][:, w], row(yn_hi, b))]).then_inc(done, 1)

            def spread(pair, b):
                pe.wait_ge(h_ready, 2 * pair + b - 1)
                nc.tensor.matmul(bank[6 + b][:], pick[:, bass.ds((pair - 1) * P, P)], row(comb_t, b),
                                 start=True, stop=True).then_inc(spread_done, 1)

            def down(pair, b, slot, start=False, stop=False):
                pe.wait_ge(h_lo_ready, 2 * pair + b + 1)
                w = slice(W_GU, W_PAIR)
                wide(bank[b][:], [(w_hi[slot][:, w], h_hi[b][:]), (w_hi[slot][:, w], h_lo[b][:]),
                                  (w_lo[slot][:, w], h_hi[b][:])], start=start, stop=stop).then_inc(down_done, 1)

            pe.wait_ge(gu_lo_ready, 1)
            for b in range(B):
                gate_up(0, b, 0)
            for b in range(B):
                pe.wait_ge(comb3_ready, b + 1)
                if b == 0:
                    pe.wait_ge(consts, 5)
                for t in range(TPB):
                    last = nc.tensor.transpose(
                        bank[6 + b][:].bitcast(BF16)[0:PARTS * EXPERTS, SEQ + t * P:SEQ + (t + 1) * P],
                        comb3[:, b, t].rearrange("p k e -> p (k e)"), ident_bf[:])
                last.then_inc(comb_t_done, 1)

            def pair_steps(pair, slot, first=False):
                pe.wait_ge(gu_lo_ready, pair + 1)
                for b in range(B):
                    gate_up(pair, b, slot)
                    if first:
                        pe.wait_ge(comb_t_ready, b + 1)
                    spread(pair, b)
                    if b == 0:
                        pe.wait_ge(d_lo_ready, pair)
                    down(pair - 1, b, 1 - slot, start=first)
                    if first:
                        for t in range(TPB):
                            nc.tensor.matmul(bank[b][:, t * P:(t + 1) * P], tile_of(y, b, t), ident[:],
                                             start=False, stop=False)

            pe.wait_ge(consts, 6)
            pair_steps(1, 1, first=True)
            pair_steps(2, 0)
            with pe.Fori(1, LOOPS) as it:
                for s in range(2):
                    pair_steps(it * 2 + (1 + s), 1 - s)
            pair_steps(PAIRS - 1, 1)
            pair_steps(PAIRS, 0)
            pe.wait_ge(d_lo_ready, PAIRS + 1)
            for b in range(B):
                down(PAIRS, b, 0, stop=True)


def kernel(**inputs):
    import numpy as _np
    import concourse.bacc as _bacc
    from concourse import mybir as _mybir
    from concourse.bass_utils import run_bass_kernel_spmd as _run

    a = {k.removeprefix("L0_"): _np.asarray(v) for k, v in inputs.items()}
    x_tok = a["x"].reshape(B * TPB, P, P).transpose(1, 0, 2).reshape(P, T)
    ctx_t = a["ctx_1024"].transpose(2, 0, 1)
    over = lambda v: _np.broadcast_to(v[None, :], (P, v.shape[0]))
    small = {
        "ctx4T": _np.broadcast_to(ctx_t[:, :, None, :], (P, B, HPG, KEYS)).reshape(P, B * P),
        "wk": a["xattn_Wk"], "wv": a["xattn_Wv"], "wq": a["xattn_Wq"], "wo": a["xattn_Wo"],
        "bq": a["xattn_bq"][:, None], "bk": a["xattn_bk"][:, None],
        "bv": over(a["xattn_bv"]), "bo": over(a["xattn_bo"]),
        "gate": a["ffn_gate_weight"].T, "ebias": over(a["ffn_e_score_correction_bias"]),
    }
    gu = a["ffn_experts_gate_up"].reshape(PAIRS, 2, 2, INTER, P).transpose(4, 0, 2, 1, 3).reshape(P, PAIRS, W_GU)
    down = a["ffn_experts_down"].transpose(0, 2, 1).reshape(PAIRS, P, P).transpose(1, 0, 2)
    shared = _np.concatenate([a["ffn_shared_gate_w"].T, a["ffn_shared_up_w"].T, a["ffn_shared_down_w"].T], axis=1)
    weights = _np.concatenate([shared, _np.concatenate([gu, down], axis=2).reshape(P, PAIRS * W_PAIR)], axis=1)
    arrays = {
        "x_tok": x_tok,
        "small": _np.concatenate([small[name] for name, _ in SMALL], axis=1),
        "weights": weights,
    }
    arrays = {k: _np.ascontiguousarray(v) for k, v in arrays.items()}

    nc = _bacc.Bacc("TRN2", target_bir_lowering=False, num_devices=1)
    aps = [nc.dram_tensor(f"{k}_dram", v.shape, _mybir.dt.from_np(v.dtype), kind="ExternalInput").ap()
           for k, v in arrays.items()]
    out_t = nc.dram_tensor("out_t_dram", (P, T), _mybir.dt.float32, kind="ExternalOutput").ap()
    xattn_moe(nc, *aps, out_t)
    r = _run(nc, [{f"{k}_dram": v for k, v in arrays.items()}], core_ids=[0])
    return r.results[0]["out_t_dram"].T.reshape(B, SEQ, P)
```

```python
from contextlib import ExitStack

import concourse.bass as bass
from concourse import mybir

F32 = mybir.dt.float32
F32R = mybir.dt.float32r
BF16 = mybir.dt.bfloat16
ALU = mybir.AluOpType
ACT = mybir.ActivationFunctionType
AXIS_X = mybir.AxisListType.X

P = 128
B = 2
SEQ = 512
TPB = SEQ // P
T = B * SEQ
HEADS, HD, KEYS = 16, 8, 32
HPG = P // KEYS
HG = HEADS // HPG
VE_W = HPG * HD + HPG
EXPERTS, GROUPS, TOP_GROUPS, TOP_K = 32, 8, 4, 6
EPG = EXPERTS // GROUPS
ROUTE_SCALE = 2.5
INTER = 64
PAIRS = EXPERTS // 2
W_GU, W_D = 2 * P, P
W_PAIR = W_GU + W_D
K = 6
LOOPS = (PAIRS - K - 2) // 2
WARM = 9
UNITS = B * (PAIRS + 1)
PARTS = 3
W_CUTS = [0, 3, K, 11, PAIRS + 1]
EPS = 1e-5
SENTINEL = -3.0e38
TAKEN = 3.0e38

SMALL = [("ctx4T", B * P), ("wk", P), ("wv", P), ("wq", P), ("wo", P), ("bq", 1), ("bk", 1),
         ("bv", P), ("bo", P), ("gate", EXPERTS), ("ebias", EXPERTS)]


def columns(names):
    at, where = 0, {}
    for name, n in names:
        where[name] = (at, at + n)
        at += n
    return where, at


SMALL_AT, SMALL_W = columns(SMALL)


def xattn_moe(nc, x_tok, small_in, weights_in, out_t):
    ctx = ExitStack()
    with ctx:
        def sb(name, shape, dt=F32):
            return ctx.enter_context(nc.sbuf_tensor(name, shape, dt))

        def sem(name):
            return ctx.enter_context(nc.semaphore(name))

        x = sb("x", [P, T])
        small = sb("small", [P, SMALL_W])
        raw_w = sb("raw_w", [P, (PAIRS + 1) * W_PAIR])

        def part(name):
            return small[:, SMALL_AT[name][0]:SMALL_AT[name][1]]

        eps_col = sb("eps_col", [P, 1])
        act_scratch = sb("act_scratch", [P, 1])
        warm = sb("warm", [P, SEQ], BF16)
        pool_scratch = sb("pool_scratch", [P, 1])
        ident = sb("ident", [P, P])
        ident_bf = sb("ident_bf", [P, P], BF16)
        head_of_row = sb("head_of_row", [P, HEADS])
        local_head = sb("local_head", [P, HPG, HD])
        neg_pick = sb("neg_pick", [HEADS, HG, P])
        neg_pick_r = sb("neg_pick_r", [HEADS, HG, P], F32R)
        pick = sb("pick", [PARTS * EXPERTS, PAIRS * P], BF16)

        k_hi = sb("k_hi", [P, B * KEYS], F32R)
        k_lo = sb("k_lo", [P, B * KEYS])
        kblk_hi = sb("kblk_hi", [P, B, HEADS, KEYS], F32R)
        kblk_lo = sb("kblk_lo", [P, B, HEADS, KEYS], F32R)
        v_rep = sb("v_rep", [P, B, P])
        v_ext = sb("v_ext", [P, B, HG, VE_W])
        wq_hi = sb("wq_hi", [P, P], F32R)
        wq_lo = sb("wq_lo", [P, P], F32R)
        stats = sb("stats", [P, B * TPB, 6])
        mv = sb("mv", [P, B * TPB, 2])
        std = sb("std", [P, B * TPB])
        rstd = sb("rstd", [P, B * TPB])
        xn = sb("xn", [P, T])
        xb = sb("xb", [P, T])
        xn_hi = sb("xn_hi", [P, T], F32R)
        xn_lo = sb("xn_lo", [P, T], F32R)
        q_hi = sb("q_hi", [P, T], F32R)
        q_lo = sb("q_lo", [P, T], F32R)
        smax = sb("smax", [P, B * TPB, HEADS])
        smax_t = sb("smax_t", [HEADS, T], F32R)
        probs = sb("probs", [P, B, HG, SEQ])
        rden = sb("rden", [P, B * TPB, HG, HPG])
        att = sb("att", [P, T])
        att_t = sb("att_t", [P, T])
        y = sb("y", [P, T])

        stats2 = sb("stats2", [P, B * TPB, 6])
        mv2 = sb("mv2", [P, B * TPB, 2])
        rstd2 = sb("rstd2", [P, B * TPB])
        yn = sb("yn", [P, T])
        yn_hi = sb("yn_hi", [P, T], F32R)
        yn_lo = sb("yn_lo", [P, T], F32R)
        gate_hi = sb("gate_hi", [P, EXPERTS], F32R)
        gate_lo = sb("gate_lo", [P, EXPERTS], F32R)
        score_t = sb("score_t", [EXPERTS, T])
        sfc = sb("sfc", [P, B, TPB, EXPERTS])
        g_pad = GROUPS + TOP_GROUPS
        e_pad = EXPERTS + 8 - TOP_K
        g_max = sb("g_max", [P, B, TPB, g_pad])
        g_top = sb("g_top", [P, B, TPB, 8])
        g_mark = sb("g_mark", [P, B, TPB, g_pad])
        g_sel = sb("g_sel", [P, B, TPB, GROUPS])
        masked = sb("masked", [P, B, TPB, e_pad])
        e_top = sb("e_top", [P, B, TPB, 8])
        e_mark = sb("e_mark", [P, B, TPB, e_pad])
        chosen = sb("chosen", [P, B, TPB, EXPERTS])
        ch_sum = sb("ch_sum", [P, B, TPB])
        ch_sc = sb("ch_sc", [P, B, TPB])
        ch_rec = sb("ch_rec", [P, B, TPB])
        comb = sb("comb", [P, B, TPB, EXPERTS])
        comb_r1 = sb("comb_r1", [P, B, TPB, EXPERTS])
        comb3 = sb("comb3", [P, B, TPB, PARTS, EXPERTS], BF16)
        comb_t = sb("comb_t", [PARTS * EXPERTS, T], BF16)

        r_hi = [sb(f"r_hi{p}", [P, W_PAIR], F32R) for p in range(K)]
        r_lo = [sb(f"r_lo{p}", [P, W_PAIR], F32R) for p in range(K)]
        w_hi = [sb(f"w_hi{s}", [P, W_PAIR], F32R) for s in range(2)]
        w_lo = [sb(f"w_lo{s}", [P, W_PAIR], F32R) for s in range(2)]
        act_g = [sb(f"act_g{b}", [P, SEQ]) for b in range(B)]
        gu = [sb(f"gu{b}", [P, SEQ]) for b in range(B)]
        h = [sb(f"h{b}", [P, SEQ]) for b in range(B)]
        h_hi = [sb(f"h_hi{b}", [P, SEQ], F32R) for b in range(B)]
        h_lo = [sb(f"h_lo{b}", [P, SEQ], F32R) for b in range(B)]
        result = sb("result", [P, T])

        bank = [ctx.enter_context(nc.psum_tensor(f"bank{i}", [P, SEQ], F32)) for i in range(8)]
        kv_ps = bank[6]

        x_in = [sem(f"x_in{b}") for b in range(B)]
        small_in_s = sem("small_in")
        w_in = [sem(f"w_in{n}") for n in range(len(W_CUTS) - 1)]
        out_done = sem("out_done")
        eps_set = sem("eps_set")
        warm_set = sem("warm_set")
        ident_set = sem("ident_set")
        heads_set = sem("heads_set")
        neg_pick_set = sem("neg_pick_set")
        pads_set = sem("pads_set")
        pick_set = sem("pick_set")
        xb_ready = sem("xb_ready")
        pool_step = sem("pool_step")
        kblk_lo_ready = sem("kblk_lo_ready")
        vext_ready = sem("vext_ready")
        h_lo_ready = sem("h_lo_ready")
        std_ready = sem("std_ready")
        smax_t_ready = sem("smax_t_ready")
        r_hi_ready = sem("r_hi_ready")
        k_hi_ready = sem("k_hi_ready")
        table = sem("table")
        xn_hi_ready = sem("xn_hi_ready")
        q_hi_ready = sem("q_hi_ready")
        probs_ready = sem("probs_ready")
        att_t_ready = sem("att_t_ready")
        yn_hi_ready = sem("yn_hi_ready")
        sigmoid_ready = sem("sigmoid_ready")
        comb_t_ready = sem("comb_t_ready")
        silu_ready = sem("silu_ready")
        h_hi_ready = sem("h_hi_ready")
        gu_hi_ready = sem("gu_hi_ready")
        d_hi_ready = sem("d_hi_ready")
        vec_step = sem("vec_step")
        kv_read = sem("kv_read")
        small_hi_ready = sem("small_hi_ready")
        var_ready = sem("var_ready")
        xn_ready = sem("xn_ready")
        xn_lo_ready = sem("xn_lo_ready")
        q_lo_ready = sem("q_lo_ready")
        smax_ready = sem("smax_ready")
        kblk_hi_ready = sem("kblk_hi_ready")
        r_lo_ready = sem("r_lo_ready")
        att_ready = sem("att_ready")
        y_ready = sem("y_ready")
        yn_ready = sem("yn_ready")
        yn_lo_ready = sem("yn_lo_ready")
        comb3_ready = sem("comb3_ready")
        gu_ready = sem("gu_ready")
        h_ready = sem("h_ready")
        gu_lo_ready = sem("gu_lo_ready")
        d_lo_ready = sem("d_lo_ready")
        result_ready = [sem(f"result_ready{b}") for b in range(B)]
        kv_done = sem("kv_done")
        xn_t_done = sem("xn_t_done")
        q_done = sem("q_done")
        score_done = sem("score_done")
        smax_t_done = sem("smax_t_done")
        score_t_done = sem("score_t_done")
        av_done = sem("av_done")
        att_t_done = sem("att_t_done")
        proj_done = sem("proj_done")
        yn_t_done = sem("yn_t_done")
        logits_done = sem("logits_done")
        score_back = sem("score_back")
        comb_t_done = sem("comb_t_done")
        gate_done = sem("gate_done")
        up_done = sem("up_done")
        spread_done = sem("spread_done")
        down_done = sem("down_done")

        def tile_of(tensor, b, t, w=P):
            i = b * TPB + t
            return tensor[:, i * w:(i + 1) * w]

        def row(tensor, b):
            return tensor[:, b * SEQ:(b + 1) * SEQ]

        def keys_of(keys, b):
            return keys[:, b * KEYS:(b + 1) * KEYS].bitcast(F32).unsqueeze(1).broadcast_to([P, HEADS, KEYS])

        def router_scores(b):
            return bank[6 + b][:, SEQ // 2:SEQ // 2 + TPB * EXPERTS].rearrange("p (t e) -> p t e", t=TPB)

        def head_mask():
            return head_of_row[:].unsqueeze(2).broadcast_to([P, HEADS, KEYS])

        block = ctx.enter_context(nc.Block())

        @block.sync
        def _(sp):
            for b in range(B):
                sp.dma_start(row(x, b), x_tok[:, b * SEQ:(b + 1) * SEQ]).then_inc(x_in[b], 16)
            for n, (lo, hi) in enumerate(zip(W_CUTS, W_CUTS[1:])):
                sp.dma_start(raw_w[:, lo * W_PAIR:hi * W_PAIR],
                             weights_in[:, lo * W_PAIR:hi * W_PAIR]).then_inc(w_in[n], 16)
            for b in range(B):
                sp.wait_ge(result_ready[b], 1)
                sp.dma_start(out_t[:, b * SEQ:(b + 1) * SEQ], row(result, b)).then_inc(out_done, 16)
            sp.wait_ge(out_done, 16 * B)

        @block.gpsimd
        def _(pool):
            steps = [0]

            def step(ins):
                steps[0] += 1
                ins.then_inc(pool_step, 1)
                pool.wait_ge(pool_step, steps[0])

            nc.gpsimd.memset(eps_col[:], EPS).then_inc(eps_set, 1)
            nc.gpsimd.memset(warm[:], 0.0).then_inc(warm_set, 1)
            step(nc.gpsimd.memset(ident[:], 0.0))
            nc.gpsimd.affine_select(out=ident[:], in_=ident[:], compare_op=ALU.not_equal, fill=1.0, base=0,
                                    pattern=[[-1, P]], channel_multiplier=1).then_inc(ident_set, 1)
            step(nc.gpsimd.memset(head_of_row[:], 1.0))
            step(nc.gpsimd.affine_select(out=head_of_row[:], in_=head_of_row[:], compare_op=ALU.is_ge, fill=0.0,
                                         base=0, pattern=[[-HD, HEADS]], channel_multiplier=1))
            nc.gpsimd.affine_select(out=head_of_row[:], in_=head_of_row[:], compare_op=ALU.is_ge, fill=0.0,
                                    base=HD - 1, pattern=[[HD, HEADS]], channel_multiplier=-1).then_inc(heads_set, 1)
            step(nc.gpsimd.memset(local_head[:], 1.0))
            step(nc.gpsimd.affine_select(out=local_head[:], in_=local_head[:], compare_op=ALU.is_ge, fill=0.0,
                                         base=0, pattern=[[-KEYS, HPG], [0, HD]], channel_multiplier=1))
            step(nc.gpsimd.affine_select(out=local_head[:], in_=local_head[:], compare_op=ALU.is_ge, fill=0.0,
                                         base=KEYS - 1, pattern=[[KEYS, HPG], [0, HD]], channel_multiplier=-1))
            step(nc.gpsimd.memset(neg_pick[:], -1.0))
            nc.gpsimd.affine_select(out=neg_pick_r[:].rearrange("p g (h k) -> p g h k", h=HPG),
                                    in_=neg_pick[:].rearrange("p g (h k) -> p g h k", h=HPG),
                                    compare_op=ALU.is_equal, fill=0.0, base=0,
                                    pattern=[[-HPG, HG], [-1, HPG], [0, KEYS]],
                                    channel_multiplier=1).then_inc(neg_pick_set, 1)
            pool.wait_ge(heads_set, 1)
            pool.wait_ge(k_hi_ready, 1)
            for b in range(B):
                nc.gpsimd.tensor_tensor(kblk_hi[:, b], keys_of(k_hi, b), head_mask(),
                                        ALU.mult).then_inc(kblk_hi_ready, 1)
            pool.wait_ge(kv_read, 1)
            for b in range(B):
                nc.gpsimd.tensor_tensor(kblk_lo[:, b], keys_of(k_lo, b), head_mask(),
                                        ALU.mult).then_inc(kblk_lo_ready, 1)
            pool.wait_ge(kv_read, 2)
            for b in range(B):
                mask = local_head[:].rearrange("p h d -> p (h d)").unsqueeze(1).broadcast_to([P, HG, HPG * HD])
                nc.gpsimd.tensor_tensor(v_ext[:, b, :, 0:HPG * HD],
                                        v_rep[:, b].rearrange("p (g c) -> p g c", g=HG), mask,
                                        ALU.mult).then_inc(vext_ready, 1)
                nc.gpsimd.tensor_copy(v_ext[:, b, :, HPG * HD:VE_W],
                                      local_head[:, :, 0].unsqueeze(1).broadcast_to([P, HG, HPG])
                                      ).then_inc(vext_ready, 1)
            pool.wait_ge(small_in_s, 16)
            for b in range(B):
                pool.wait_ge(x_in[b], 16)
                nc.gpsimd.tensor_tensor(row(xb, b).rearrange("p (t f) -> p t f", t=TPB),
                                        row(x, b).rearrange("p (t f) -> p t f", t=TPB),
                                        part("bo").unsqueeze(1).broadcast_to([P, TPB, P]),
                                        ALU.add).then_inc(xb_ready, 1)
            nc.gpsimd.memset(g_max[:], SENTINEL).then_inc(pads_set, 1)
            nc.gpsimd.memset(masked[:], SENTINEL).then_inc(pads_set, 1)
            pool.wait_ge(ident_set, 1)
            nc.gpsimd.tensor_copy(ident_bf[:], ident[:]).then_inc(ident_set, 1)
            step(nc.gpsimd.memset(pick[:], 0.0))
            for k in range(PARTS):
                step(nc.gpsimd.affine_select(out=pick[:], in_=pick[:], compare_op=ALU.not_equal, fill=1.0,
                                             base=-k * EXPERTS, pattern=[[-2, PAIRS], [-1, 2], [0, INTER]],
                                             channel_multiplier=1))
            nc.gpsimd.memset(pool_scratch[:], 0.0).then_inc(pick_set, 1)

            def low_part(n, j):
                pool.wait_ge(h_hi_ready, n + 1)
                nc.gpsimd.tensor_tensor(h_lo[j][:], h[j][:], h_hi[j][:].bitcast(F32),
                                        ALU.subtract).then_inc(h_lo_ready, 1)

            for n in range(2 * K + B):
                low_part(n, n % 2)
            with pool.Fori(0, LOOPS) as it:
                for u in range(2 * B):
                    low_part(it * (2 * B) + (2 * K + B + u), u % 2)
            for n in range(UNITS - 2 * B, UNITS):
                low_part(n, n % 2)

        @block.scalar
        def _(act):
            act.dma_start(small[:], small_in[:, :]).then_inc(small_in_s, 16)

            def deviation(n, m, b):
                act.wait_ge(var_ready, n)
                nc.scalar.activation(std[:, b * TPB:(b + 1) * TPB], m[:, b * TPB:(b + 1) * TPB, 1], ACT.Sqrt,
                                     bias=eps_col[:]).then_inc(std_ready, 1)

            def evacuate(dst, src, wait, n, ready):
                act.wait_ge(wait, n)
                nc.scalar.activation(dst, src, ACT.Copy).then_inc(ready, 1)

            def query(b):
                act.wait_ge(q_done, b + 1)
                nc.scalar.activation(row(q_hi, b), bank[2 + b][:], ACT.Identity,
                                     bias=part("bq")).then_inc(q_hi_ready, 1)

            def exps(b, g):
                act.wait_ge(score_t_done, b * HG + g + 1)
                nc.scalar.activation(probs[:, b, g], bank[4 + g % 2][:], ACT.Exp,
                                     scale=HD ** -0.5).then_inc(probs_ready, 1)

            def sigmoid(b):
                act.wait_ge(logits_done, b + 1)
                nc.scalar.activation(score_t[:, b * SEQ:(b + 1) * SEQ], bank[6 + b][0:EXPERTS, :],
                                     ACT.Sigmoid).then_inc(sigmoid_ready, 1)

            tables = [0]

            def load_table(func):
                if tables[0]:
                    act.wait_ge(table, tables[0])
                tables[0] += 1
                nc.scalar.activation(act_scratch[:], eps_col[:], func).then_inc(table, 1)

            def weights_high(dst, pair, at, n, ready):
                nc.scalar.activation(dst, raw_w[:, bass.ds(pair * W_PAIR + at, n)], ACT.Copy).then_inc(ready, 1)

            def resident_high(pair):
                if pair in W_CUTS:
                    act.wait_ge(w_in[W_CUTS.index(pair)], 16)
                weights_high(r_hi[pair][:], pair, 0, W_PAIR, r_hi_ready)

            def silu(n, b, j, first=False):
                act.wait_ge(gate_done, n + 1)
                if not first:
                    act.wait_ge(gu_ready, n - 1)
                nc.scalar.activation(act_g[j][:], bank[2 + b][:], ACT.Silu).then_inc(silu_ready, 1)

            def high_part(n, j, first=False):
                act.wait_ge(h_ready, n + 1)
                if not first:
                    act.wait_ge(down_done, n - 1)
                nc.scalar.activation(h_hi[j][:], h[j][:], ACT.Copy).then_inc(h_hi_ready, 1)

            act.wait_ge(eps_set, 1)
            load_table(ACT.Sqrt)
            deviation(1, mv, 0)
            act.wait_ge(kv_done, 1)
            nc.scalar.activation(k_hi[:], kv_ps[:, 0:B * KEYS], ACT.Identity, bias=part("bk")).then_inc(k_hi_ready, 1)
            evacuate(row(xn_hi, 0), bank[0][:], xn_t_done, 1, xn_hi_ready)
            deviation(2, mv, 1)
            load_table(ACT.Exp)
            query(0)
            evacuate(row(xn_hi, 1), bank[1][:], xn_t_done, 2, xn_hi_ready)
            query(1)
            resident_high(0)
            evacuate(row(smax_t, 0), bank[0][0:HEADS, :], smax_t_done, 1, smax_t_ready)
            for g in range(HG):
                exps(0, g)
            resident_high(1)
            evacuate(row(smax_t, 1), bank[1][0:HEADS, :], smax_t_done, 2, smax_t_ready)
            resident_high(2)
            exps(1, 0)
            exps(1, 1)
            evacuate(row(att_t, 0), bank[2][:], att_t_done, 1, att_t_ready)
            exps(1, 2)
            exps(1, 3)
            load_table(ACT.Sqrt)
            deviation(3, mv2, 0)
            load_table(ACT.Sigmoid)
            evacuate(row(yn_hi, 0), bank[2][:], yn_t_done, 1, yn_hi_ready)
            sigmoid(0)
            load_table(ACT.Silu)
            resident_high(3)
            silu(0, 0, 0, first=True)
            evacuate(row(att_t, 1), bank[3][:], att_t_done, 2, att_t_ready)
            silu(1, 0, 1, first=True)
            high_part(0, 0, first=True)
            evacuate(row(comb_t, 0), bank[6][:].bitcast(BF16)[0:PARTS * EXPERTS, 0:SEQ],
                     comb_t_done, 1, comb_t_ready)
            deviation(4, mv2, 1)
            silu(2, 0, 0)
            high_part(1, 1, first=True)
            resident_high(4)
            evacuate(row(yn_hi, 1), bank[3][:], yn_t_done, 2, yn_hi_ready)
            silu(3, 0, 1)
            high_part(2, 0)
            sigmoid(1)
            resident_high(5)
            silu(4, 0, 0)
            high_part(3, 1)
            silu(5, 0, 1)
            high_part(4, 0)
            for p in range(K):
                silu(K + p, 1, p % 2)
                high_part(K + p - 1, (p - 1) % 2)
                if p == 0:
                    evacuate(row(comb_t, 1), bank[7][:].bitcast(BF16)[0:PARTS * EXPERTS, 0:SEQ],
                             comb_t_done, 2, comb_t_ready)
                if p == K - 1:
                    act.wait_ge(w_in[W_CUTS.index(K)], 16)
                    weights_high(w_hi[K % 2][:, 0:W_GU], K, 0, W_GU, gu_hi_ready)
            for arrived in w_in[W_CUTS.index(K) + 1:]:
                act.wait_ge(arrived, 16)

            def pair_steps(pair, slot, last=False):
                n = pair * B
                if not last:
                    act.wait_ge(up_done, n)
                    weights_high(w_hi[1 - slot][:, 0:W_GU], pair + 1, 0, W_GU, gu_hi_ready)
                silu(n, 0, 0)
                act.wait_ge(h_ready, n)
                nc.scalar.activation(h_hi[1][:], h[1][:], ACT.Copy).then_inc(h_hi_ready, 1)
                silu(n + 1, 1, 1)
                weights_high(w_hi[slot][:, W_GU:W_PAIR], pair, W_GU, W_D, d_hi_ready)
                high_part(n, 0)

            pair_steps(K, K % 2)
            with act.Fori(0, LOOPS) as it:
                for s in range(2):
                    pair_steps(it * 2 + (K + 1 + s), (K + 1 + s) % 2)
            pair_steps(PAIRS - 1, (PAIRS - 1) % 2)
            pair_steps(PAIRS, PAIRS % 2, last=True)
            high_part(UNITS - 1, 1)
            act.wait_ge(down_done, UNITS - 1)
            nc.scalar.activation(row(result, 0), bank[0][:], ACT.Copy).then_inc(result_ready[0], 1)

        @block.vector
        def _(dve):
            steps = [0]

            def mark(ins):
                steps[0] += 1
                ins.then_inc(vec_step, 1)

            def settle():
                dve.wait_ge(vec_step, steps[0])

            def step(ins):
                mark(ins)
                settle()

            def moments(src, st, out, b):
                for t in range(TPB):
                    mark(nc.vector.bn_stats(st[:, b * TPB + t], tile_of(src, b, t)))
                settle()
                for t in range(TPB):
                    last = nc.vector.bn_aggr(out[:, b * TPB + t], st[:, b * TPB + t])
                last.then_inc(var_ready, 1)

            def normalise(src, m, r, out, b, n, ready):
                v = slice(b * TPB, (b + 1) * TPB)
                dve.wait_ge(std_ready, n)
                step(nc.vector.reciprocal(r[:, v], std[:, v]))
                for t in range(TPB):
                    i = b * TPB + t
                    nc.vector.tensor_scalar(tile_of(out, b, t), tile_of(src, b, t), m[:, i, 0:1], r[:, i:i + 1],
                                            ALU.subtract, ALU.mult).then_inc(ready, 1)

            def low_of(lo, hi, src, b, hi_ready, ready):
                dve.wait_ge(hi_ready, b + 1)
                nc.vector.tensor_tensor(row(lo, b), src[:], row(hi, b).bitcast(F32), ALU.subtract).then_inc(ready, 1)

            def query_low(b):
                dve.wait_ge(q_hi_ready, b + 1)
                nc.vector.scalar_tensor_tensor(row(q_lo, b), bank[2 + b][:], part("bq"), row(q_hi, b).bitcast(F32),
                                               ALU.add, ALU.subtract).then_inc(q_lo_ready, 1)

            def score_max(b, t):
                i = b * TPB + t
                dve.wait_ge(score_done, i + 1)
                nc.vector.tensor_reduce(out=smax[:, i], in_=bank[6 + t % 2][:].rearrange("p (h k) -> p h k", k=KEYS),
                                        op=ALU.max, axis=AXIS_X).then_inc(smax_ready, 1)

            def attended(b, half):
                where = bank[b] if half else bank[2 + b]
                i = b * TPB + 2 * half
                dve.wait_ge(av_done, b * 2 + half + 1)
                sums = where[:, 0:2 * HG * VE_W].rearrange("p (g c) -> p g c", c=VE_W)
                dens = rden[:, i:i + 2].rearrange("p t g h -> p (t g) h")
                step(nc.vector.reciprocal(dens, sums[:, :, HPG * HD:VE_W]))
                nc.vector.tensor_tensor(
                    att[:, i * P:(i + 2) * P].rearrange("p (g h d) -> p g h d", h=HPG, d=HD),
                    sums[:, :, 0:HPG * HD].rearrange("p g (h d) -> p g h d", d=HD),
                    dens.unsqueeze(3).broadcast_to([P, 2 * HG, HPG, HD]), ALU.mult).then_inc(att_ready, 1)

            def residual(b):
                dve.wait_ge(proj_done, b + 1)
                dve.wait_ge(xb_ready, b + 1)
                nc.vector.tensor_tensor(row(y, b), bank[b][:], row(xb, b), ALU.add).then_inc(y_ready, 1)
                dve.wait_ge(y_ready, b + 1)
                moments(y, stats2, mv2, b)

            def route_groups(b):
                dve.wait_ge(score_back, b + 1)
                step(nc.vector.tensor_tensor(sfc[:, b], router_scores(b),
                                             part("ebias").unsqueeze(1).broadcast_to([P, TPB, EXPERTS]), ALU.add))
                step(nc.vector.tensor_reduce(out=g_max[:, b, :, 0:GROUPS],
                                             in_=sfc[:, b].rearrange("p t (g e) -> p t g e", e=EPG),
                                             op=ALU.max, axis=AXIS_X))
                for t in range(TPB):
                    mark(nc.vector.max(g_top[:, b, t], g_max[:, b, t, 0:GROUPS]))
                settle()
                step(nc.vector.memset(g_top[:, b, :, TOP_GROUPS:8], SENTINEL))
                for t in range(TPB):
                    mark(nc.vector.match_replace(out=g_mark[:, b, t], in_to_replace=g_top[:, b, t],
                                                 in_values=g_max[:, b, t], imm_value=TAKEN))

            def route_experts(b):
                settle()
                step(nc.vector.tensor_scalar(g_sel[:, b], g_mark[:, b, :, 0:GROUPS], TAKEN, None, ALU.is_equal))
                step(nc.vector.tensor_tensor(
                    masked[:, b, :, 0:EXPERTS].rearrange("p t (g e) -> p t g e", e=EPG),
                    sfc[:, b].rearrange("p t (g e) -> p t g e", e=EPG),
                    g_sel[:, b].unsqueeze(3).broadcast_to([P, TPB, GROUPS, EPG]), ALU.mult))
                for t in range(TPB):
                    mark(nc.vector.max(e_top[:, b, t], masked[:, b, t, 0:EXPERTS]))
                settle()
                step(nc.vector.memset(e_top[:, b, :, TOP_K:8], SENTINEL))
                for t in range(TPB):
                    mark(nc.vector.match_replace(out=e_mark[:, b, t], in_to_replace=e_top[:, b, t],
                                                 in_values=masked[:, b, t], imm_value=TAKEN))

            def route_weights(b):
                settle()
                step(nc.vector.scalar_tensor_tensor(chosen[:, b], e_mark[:, b, :, 0:EXPERTS], TAKEN, router_scores(b),
                                                    ALU.is_equal, ALU.mult))
                step(nc.vector.tensor_reduce(out=ch_sum[:, b], in_=chosen[:, b], op=ALU.add, axis=AXIS_X))
                step(nc.vector.tensor_scalar(ch_sc[:, b], ch_sum[:, b], 1e-20, 1.0 / ROUTE_SCALE, ALU.add, ALU.mult))
                step(nc.vector.reciprocal(ch_rec[:, b], ch_sc[:, b]))
                mark(nc.vector.tensor_tensor(comb[:, b], chosen[:, b],
                                             ch_rec[:, b].unsqueeze(2).broadcast_to([P, TPB, EXPERTS]), ALU.mult))

            def route_parts(b):
                settle()
                step(nc.vector.tensor_copy(comb3[:, b, :, 0], comb[:, b]))
                step(nc.vector.tensor_tensor(comb_r1[:, b], comb[:, b], comb3[:, b, :, 0], ALU.subtract))
                step(nc.vector.tensor_copy(comb3[:, b, :, 1], comb_r1[:, b]))
                nc.vector.tensor_tensor(comb3[:, b, :, 2], comb_r1[:, b], comb3[:, b, :, 1],
                                        ALU.subtract).then_inc(comb3_ready, 1)

            def weights_low(dst, hi, pair, at, n, hi_ready, count, ready):
                dve.wait_ge(hi_ready, count)
                nc.vector.tensor_tensor(dst, raw_w[:, bass.ds(pair * W_PAIR + at, n)], hi.bitcast(F32),
                                        ALU.subtract).then_inc(ready, 1)

            def resident_low(pair):
                if pair in W_CUTS:
                    dve.wait_ge(w_in[W_CUTS.index(pair)], 16)
                weights_low(r_lo[pair][:], r_hi[pair][:], pair, 0, W_PAIR, r_hi_ready, pair + 1, r_lo_ready)

            def gated(n, b, j, first=False):
                dve.wait_ge(silu_ready, n + 1)
                dve.wait_ge(up_done, n + 1)
                if not first:
                    dve.wait_ge(h_ready, n - 1)
                nc.vector.tensor_tensor(gu[j][:], bank[4 + b][:], act_g[j][:], ALU.mult).then_inc(gu_ready, 1)

            def weighted(n, b, j, spreads, first=False):
                dve.wait_ge(spread_done, spreads)
                dve.wait_ge(gu_ready, n + 1)
                if not first:
                    dve.wait_ge(h_lo_ready, n - 1)
                nc.vector.tensor_tensor(h[j][:], bank[6 + b][:], gu[j][:], ALU.mult).then_inc(h_ready, 1)

            def unweighted(n, j, first=False):
                dve.wait_ge(gu_ready, n + 1)
                if not first:
                    dve.wait_ge(h_lo_ready, n - 1)
                nc.vector.tensor_copy(h[j][:], gu[j][:]).then_inc(h_ready, 1)

            dve.wait_ge(x_in[0], 16)
            moments(x, stats, mv, 0)
            dve.wait_ge(small_in_s, 16)
            mark(nc.vector.tensor_copy(wq_hi[:], part("wq")))
            mark(nc.vector.tensor_copy(gate_hi[:], part("gate")))
            normalise(x, mv, rstd, xn, 0, 1, xn_ready)
            nc.vector.tensor_tensor(wq_lo[:], part("wq"), wq_hi[:].bitcast(F32), ALU.subtract).then_inc(small_hi_ready, 1)
            dve.wait_ge(x_in[1], 16)
            moments(x, stats, mv, 1)
            low_of(xn_lo, xn_hi, bank[0], 0, xn_hi_ready, xn_lo_ready)
            dve.wait_ge(k_hi_ready, 1)
            nc.vector.scalar_tensor_tensor(k_lo[:], kv_ps[:, 0:B * KEYS], part("bk"), k_hi[:].bitcast(F32),
                                           ALU.add, ALU.subtract).then_inc(kv_read, 1)
            normalise(x, mv, rstd, xn, 1, 2, xn_ready)
            nc.vector.tensor_tensor(v_rep[:], kv_ps[:, P:P + B * P].rearrange("p (b f) -> p b f", b=B),
                                    part("bv").unsqueeze(1).broadcast_to([P, B, P]), ALU.add).then_inc(kv_read, 1)
            query_low(0)
            low_of(xn_lo, xn_hi, bank[1], 1, xn_hi_ready, xn_lo_ready)
            for t in range(TPB):
                score_max(0, t)
            query_low(1)
            nc.vector.tensor_tensor(gate_lo[:], part("gate"), gate_hi[:].bitcast(F32),
                                    ALU.subtract).then_inc(small_hi_ready, 1)
            for t in range(TPB):
                score_max(1, t)
            resident_low(0)
            resident_low(1)
            attended(0, 0)
            attended(0, 1)
            resident_low(2)
            residual(0)
            normalise(y, mv2, rstd2, yn, 0, 3, yn_ready)
            low_of(yn_lo, yn_hi, bank[2], 0, yn_hi_ready, yn_lo_ready)
            attended(1, 0)
            attended(1, 1)
            dve.wait_ge(pads_set, 2)
            route_groups(0)
            route_experts(0)
            gated(0, 0, 0, first=True)
            route_weights(0)
            unweighted(0, 0, first=True)
            route_parts(0)
            gated(1, 0, 1, first=True)
            residual(1)
            weighted(1, 0, 1, 1, first=True)
            resident_low(3)
            gated(2, 0, 0)
            normalise(y, mv2, rstd2, yn, 1, 4, yn_ready)
            weighted(2, 0, 0, 2)
            resident_low(4)
            gated(3, 0, 1)
            low_of(yn_lo, yn_hi, bank[3], 1, yn_hi_ready, yn_lo_ready)
            weighted(3, 0, 1, 3)
            resident_low(5)
            gated(4, 0, 0)
            weighted(4, 0, 0, 4)
            route_groups(1)
            gated(5, 0, 1)
            route_experts(1)
            weighted(5, 0, 1, 5)
            route_weights(1)
            gated(K, 1, 0)
            unweighted(K, 0)
            route_parts(1)
            for p in range(1, K):
                gated(K + p, 1, p % 2)
                if p == K - 1:
                    dve.wait_ge(w_in[W_CUTS.index(K)], 16)
                    weights_low(w_lo[K % 2][:, 0:W_GU], w_hi[K % 2][:, 0:W_GU], K, 0, W_GU, gu_hi_ready, 1, gu_lo_ready)
                weighted(K + p, 1, p % 2, K + p - 1)
            for arrived in w_in[W_CUTS.index(K) + 1:]:
                dve.wait_ge(arrived, 16)

            def pair_steps(pair, slot, last=False):
                n = pair * B
                if not last:
                    weights_low(w_lo[1 - slot][:, 0:W_GU], w_hi[1 - slot][:, 0:W_GU], pair + 1, 0, W_GU,
                                gu_hi_ready, pair - K + 2, gu_lo_ready)
                gated(n, 0, 0)
                weighted(n, 0, 0, n - 1)
                gated(n + 1, 1, 1)
                weights_low(w_lo[slot][:, W_GU:W_PAIR], w_hi[slot][:, W_GU:W_PAIR], pair, W_GU, W_D,
                            d_hi_ready, pair - K + 1, d_lo_ready)
                weighted(n + 1, 1, 1, n)

            pair_steps(K, K % 2)
            with dve.Fori(0, LOOPS) as it:
                for s in range(2):
                    pair_steps(it * 2 + (K + 1 + s), (K + 1 + s) % 2)
            pair_steps(PAIRS - 1, (PAIRS - 1) % 2)
            pair_steps(PAIRS, PAIRS % 2, last=True)
            dve.wait_ge(down_done, UNITS)
            nc.vector.tensor_copy(row(result, 1), bank[1][:]).then_inc(result_ready[1], 1)

        @block.tensor
        def _(pe):
            def wide(out, pairs, start=True, stop=True):
                for n, (lhs_t, rhs) in enumerate(pairs):
                    last = nc.tensor.matmul(out, lhs_t, rhs, start=start and n == 0,
                                            stop=stop and n == len(pairs) - 1)
                return last

            def turn_tiles(where, src, b, ready, count, done, per_tile=0):
                for t in range(TPB):
                    if per_tile or t == 0:
                        pe.wait_ge(ready, count + per_tile * t)
                    last = nc.tensor.transpose(where[:, t * P:(t + 1) * P], tile_of(src, b, t), ident[:])
                last.then_inc(done, 1)

            def query(b):
                pe.wait_ge(xn_hi_ready, b + 1)
                pe.wait_ge(xn_lo_ready, b + 1)
                wide(bank[2 + b][:], [(wq_hi[:], row(xn_hi, b)), (wq_hi[:], row(xn_lo, b)),
                                      (wq_lo[:], row(xn_hi, b))]).then_inc(q_done, 1)

            def scores(b, t):
                i = b * TPB + t
                if t == 0:
                    pe.wait_ge(q_hi_ready, b + 1)
                    pe.wait_ge(kblk_hi_ready, b + 1)
                if i == 0:
                    pe.wait_ge(kv_read, 2)
                if i >= 2:
                    pe.wait_ge(smax_ready, i - 1)
                nc.tensor.matmul(bank[6 + t % 2][:], tile_of(q_hi, b, t), kblk_hi[:, b].rearrange("p h k -> p (h k)"),
                                 start=True, stop=True).then_inc(score_done, 1)

            def turn_max(b):
                pe.wait_ge(xn_lo_ready, b + 1)
                for t in range(TPB):
                    i = b * TPB + t
                    pe.wait_ge(smax_ready, i + 1)
                    last = nc.tensor.transpose(bank[b][0:HEADS, t * P:(t + 1) * P], smax[:, i], ident[:])
                last.then_inc(smax_t_done, 1)

            def shifted_scores(b, g):
                if g == 0:
                    pe.wait_ge(q_lo_ready, b + 1)
                    pe.wait_ge(smax_t_ready, b + 1)
                    pe.wait_ge(kblk_lo_ready, b + 1)
                if b * HG + g >= 2:
                    pe.wait_ge(probs_ready, b * HG + g - 1)
                hs = slice(g * HPG, (g + 1) * HPG)
                k_h = kblk_hi[:, b, hs].rearrange("p h k -> p (h k)")
                k_l = kblk_lo[:, b, hs].rearrange("p h k -> p (h k)")
                wide(bank[4 + g % 2][:], [(k_h, row(q_hi, b)), (k_h, row(q_lo, b)), (k_l, row(q_hi, b)),
                                          (neg_pick_r[:, g], row(smax_t, b))]).then_inc(score_t_done, 1)

            def head_sums(b):
                pe.wait_ge(vext_ready, 2 * (b + 1))
                pe.wait_ge(probs_ready, (b + 1) * HG)
                for half, where in ((0, bank[2 + b]), (1, bank[b])):
                    for t2 in range(2):
                        t = 2 * half + t2
                        for g in range(HG):
                            at = (t2 * HG + g) * VE_W
                            last = nc.tensor.matmul(where[:, at:at + VE_W], probs[:, b, g, t * P:(t + 1) * P],
                                                    v_ext[:, b, g], start=True, stop=True)
                    last.then_inc(av_done, 1)

            def project(b):
                pe.wait_ge(att_t_ready, b + 1)
                for t in range(TPB):
                    last = nc.tensor.matmul(bank[b][:, t * P:(t + 1) * P], tile_of(att_t, b, t), part("wo"),
                                            start=True, stop=True)
                last.then_inc(proj_done, 1)

            def logits(b):
                pe.wait_ge(yn_hi_ready, b + 1)
                pe.wait_ge(yn_lo_ready, b + 1)
                wide(bank[6 + b][0:EXPERTS, :], [(gate_hi[:], row(yn_hi, b)), (gate_hi[:], row(yn_lo, b)),
                                                 (gate_lo[:], row(yn_hi, b))]).then_inc(logits_done, 1)

            def turn_scores(b):
                pe.wait_ge(sigmoid_ready, b + 1)
                for t in range(TPB):
                    last = nc.tensor.transpose(router_scores(b)[:, t], tile_of(score_t, b, t), ident[0:EXPERTS, 0:EXPERTS])
                last.then_inc(score_back, 1)

            def turn_weights(b):
                pe.wait_ge(comb3_ready, b + 1)
                for t in range(TPB):
                    last = nc.tensor.transpose(
                        bank[6 + b][:].bitcast(BF16)[0:PARTS * EXPERTS, t * P:(t + 1) * P],
                        comb3[:, b, t].rearrange("p k e -> p (k e)"), ident_bf[:])
                last.then_inc(comb_t_done, 1)

            def gate_up(n, b, hi, lo, before=None):
                for where, at, waits, done in ((bank[2 + b], 0, silu_ready, gate_done),
                                               (bank[4 + b], P, gu_ready, up_done)):
                    if before is not None:
                        pe.wait_ge(waits, before + 1)
                    w = slice(at, at + P)
                    wide(where[:], [(hi[:, w], row(yn_hi, b)), (hi[:, w], row(yn_lo, b)),
                                    (lo[:, w], row(yn_hi, b))]).then_inc(done, 1)

            def spread(b, pair, before=None):
                if before is not None:
                    pe.wait_ge(h_ready, before + 1)
                nc.tensor.matmul(bank[6 + b][:], pick[:, bass.ds((pair - 1) * P, P)], row(comb_t, b),
                                 start=True, stop=True).then_inc(spread_done, 1)

            def down(n, b, j, hi, lo, start=False, stop=False):
                pe.wait_ge(h_lo_ready, n + 1)
                w = slice(W_GU, W_PAIR)
                wide(bank[b][:], [(hi[:, w], h_hi[j][:]), (hi[:, w], h_lo[j][:]), (lo[:, w], h_hi[j][:])],
                     start=start, stop=stop).then_inc(down_done, 1)
                if start:
                    for t in range(TPB):
                        nc.tensor.matmul(bank[b][:, t * P:(t + 1) * P], tile_of(y, b, t), ident[:],
                                         start=False, stop=False)

            pe.wait_ge(warm_set, 1)
            for _ in range(WARM):
                nc.tensor.matmul(bank[7][:], warm[:, 0:P], warm[:], start=True, stop=True)
            pe.wait_ge(small_in_s, 16)
            ctx_t = part("ctx4T").rearrange("p (b r k) -> p b r k", b=B, r=HPG)
            nc.tensor.matmul(kv_ps[:, 0:B * KEYS], part("wk"), ctx_t[:, :, 0, :], start=True, stop=True)
            for b in range(B):
                last = nc.tensor.matmul(kv_ps[:, P + b * P:P + (b + 1) * P], part("ctx4T")[:, b * P:(b + 1) * P],
                                        part("wv"), start=True, stop=True)
            last.then_inc(kv_done, 1)
            pe.wait_ge(ident_set, 1)
            turn_tiles(bank[0], xn, 0, xn_ready, 1, xn_t_done, per_tile=1)
            pe.wait_ge(small_hi_ready, 1)
            query(0)
            turn_tiles(bank[1], xn, 1, xn_ready, TPB + 1, xn_t_done, per_tile=1)
            scores(0, 0)
            scores(0, 1)
            query(1)
            scores(0, 2)
            scores(0, 3)
            scores(1, 0)
            scores(1, 1)
            turn_max(0)
            pe.wait_ge(neg_pick_set, 1)
            shifted_scores(0, 0)
            scores(1, 2)
            shifted_scores(0, 1)
            scores(1, 3)
            shifted_scores(0, 2)
            shifted_scores(0, 3)
            turn_max(1)
            head_sums(0)
            shifted_scores(1, 0)
            shifted_scores(1, 1)
            turn_tiles(bank[2], att, 0, att_ready, 2, att_t_done)
            shifted_scores(1, 2)
            project(0)
            shifted_scores(1, 3)
            head_sums(1)
            turn_tiles(bank[2], yn, 0, yn_ready, 1, yn_t_done, per_tile=1)
            pe.wait_ge(small_hi_ready, 2)
            logits(0)
            turn_tiles(bank[3], att, 1, att_ready, 3 + 1, att_t_done)
            turn_scores(0)
            pe.wait_ge(r_lo_ready, 1)
            gate_up(0, 0, r_hi[0], r_lo[0])
            pe.wait_ge(r_lo_ready, 2)
            gate_up(1, 0, r_hi[1], r_lo[1], before=0)
            project(1)
            pe.wait_ge(ident_set, 2)
            turn_weights(0)
            pe.wait_ge(comb_t_ready, 1)
            pe.wait_ge(pick_set, 1)
            spread(0, 1)
            for p in range(2, K):
                pe.wait_ge(r_lo_ready, p + 1)
                gate_up(p, 0, r_hi[p], r_lo[p], before=p - 1)
                spread(0, p, before=p - 1)
                down(p - 2, 0, p % 2, r_hi[p - 2], r_lo[p - 2], start=p == 2)
                if p == 2:
                    turn_tiles(bank[3], yn, 1, yn_ready, 2 * TPB, yn_t_done)
                if p == 3:
                    logits(1)
                if p == 4:
                    turn_scores(1)
            for p in range(K):
                n = K + p
                gate_up(n, 1, r_hi[p], r_lo[p], before=n - 1 if p else None)
                if p == 1:
                    turn_weights(1)
                    pe.wait_ge(comb_t_ready, 2)
                if p:
                    spread(1, p, before=n - 1 if p > 1 else None)
                q = (n - 2) % K
                down(n - 2, 1 if p >= 2 else 0, p % 2, r_hi[q], r_lo[q], start=p == 2)

            def pair_steps(pair, slot, before_hi=None, before_lo=None):
                pe.wait_ge(gu_lo_ready, pair - K + 1)
                if before_hi is None:
                    before_hi, before_lo = w_hi[1 - slot], w_lo[1 - slot]
                    pe.wait_ge(d_lo_ready, pair - K)
                for b in range(B):
                    n = pair * B + b
                    gate_up(n, b, w_hi[slot], w_lo[slot], before=n - 2)
                    spread(b, pair, before=n - 2)
                    yield_down(n - 2, b, before_hi, before_lo)

            def yield_down(n, b, hi, lo):
                down(n, b, b, hi, lo)

            pe.wait_ge(gu_lo_ready, 1)
            for b in range(B):
                n = K * B + b
                gate_up(n, b, w_hi[K % 2], w_lo[K % 2], before=n - 2)
                spread(b, K, before=n - 2)
                down(n - 2, 1, b, r_hi[K - 2 + b], r_lo[K - 2 + b])
            pair_steps(K + 1, (K + 1) % 2)
            pair_steps(K + 2, K % 2)
            with pe.Fori(1, LOOPS) as it:
                for s in range(2):
                    pair_steps(it * 2 + (K + 1 + s), (K + 1 + s) % 2)
            pair_steps(PAIRS - 1, (PAIRS - 1) % 2)
            pair_steps(PAIRS, PAIRS % 2)
            pe.wait_ge(d_lo_ready, PAIRS - K + 1)
            for b in range(B):
                down(UNITS - 2 + b, b, b, w_hi[PAIRS % 2], w_lo[PAIRS % 2], stop=True)


def kernel(**inputs):
    import numpy as _np
    import concourse.bacc as _bacc
    from concourse import mybir as _mybir
    from concourse.bass_utils import run_bass_kernel_spmd as _run

    a = {k.removeprefix("L0_"): _np.asarray(v) for k, v in inputs.items()}
    x_tok = a["x"].reshape(B * TPB, P, P).transpose(1, 0, 2).reshape(P, T)
    ctx_t = a["ctx_1024"].transpose(2, 0, 1)
    over = lambda v: _np.broadcast_to(v[None, :], (P, v.shape[0]))
    small = {
        "ctx4T": _np.broadcast_to(ctx_t[:, :, None, :], (P, B, HPG, KEYS)).reshape(P, B * P),
        "wk": a["xattn_Wk"], "wv": a["xattn_Wv"], "wq": a["xattn_Wq"], "wo": a["xattn_Wo"],
        "bq": a["xattn_bq"][:, None], "bk": a["xattn_bk"][:, None],
        "bv": over(a["xattn_bv"]), "bo": over(a["xattn_bo"]),
        "gate": a["ffn_gate_weight"].T, "ebias": over(a["ffn_e_score_correction_bias"]),
    }
    gu = a["ffn_experts_gate_up"].reshape(PAIRS, 2, 2, INTER, P).transpose(4, 0, 2, 1, 3).reshape(P, PAIRS, W_GU)
    down = a["ffn_experts_down"].transpose(0, 2, 1).reshape(PAIRS, P, P).transpose(1, 0, 2)
    shared = _np.concatenate([a["ffn_shared_gate_w"].T, a["ffn_shared_up_w"].T, a["ffn_shared_down_w"].T], axis=1)
    weights = _np.concatenate([shared, _np.concatenate([gu, down], axis=2).reshape(P, PAIRS * W_PAIR)], axis=1)
    arrays = {
        "x_tok": x_tok,
        "small": _np.concatenate([small[name] for name, _ in SMALL], axis=1),
        "weights": weights,
    }
    arrays = {k: _np.ascontiguousarray(v) for k, v in arrays.items()}

    nc = _bacc.Bacc("TRN2", target_bir_lowering=False, num_devices=1)
    aps = [nc.dram_tensor(f"{k}_dram", v.shape, _mybir.dt.from_np(v.dtype), kind="ExternalInput").ap()
           for k, v in arrays.items()]
    out_t = nc.dram_tensor("out_t_dram", (P, T), _mybir.dt.float32, kind="ExternalOutput").ap()
    xattn_moe(nc, *aps, out_t)
    r = _run(nc, [{f"{k}_dram": v for k, v in arrays.items()}], core_ids=[0])
    return r.results[0]["out_t_dram"].T.reshape(B, SEQ, P)
```

```python
from contextlib import ExitStack

import concourse.bass as bass
from concourse import mybir

F32 = mybir.dt.float32
F32R = mybir.dt.float32r
BF16 = mybir.dt.bfloat16
ALU = mybir.AluOpType
ACT = mybir.ActivationFunctionType
AXIS_X = mybir.AxisListType.X

P = 128
B = 2
SEQ = 512
TPB = SEQ // P
T = B * SEQ
HEADS, HD, KEYS = 16, 8, 32
HPG = P // KEYS
HG = HEADS // HPG
VE_W = HPG * HD + HPG
EXPERTS, GROUPS, TOP_GROUPS, TOP_K = 32, 8, 4, 6
EPG = EXPERTS // GROUPS
ROUTE_SCALE = 2.5
INTER = 64
PAIRS = EXPERTS // 2
W_GU, W_D = 2 * P, P
W_PAIR = W_GU + W_D
K = 6
LOOPS = (PAIRS - K - 2) // 2
SPREAD_BY_DMA = PAIRS + 1 - (K + 2)
WARM = 9
UNITS = B * (PAIRS + 1)
AHEAD = B * K
SPREAD_BEHIND = [(AHEAD - 3, AHEAD - 2), (AHEAD - 1, AHEAD), (AHEAD + 1, AHEAD + 2), (AHEAD + 3,)]
PARTS = 3
W_CUTS = [0, 3, K, 11, PAIRS + 1]
EPS = 1e-5
SENTINEL = -3.0e38
TAKEN = 3.0e38

SMALL = [("ctx4T", B * P), ("wk", P), ("wv", P), ("wq", P), ("wo", P), ("bq", 1), ("bk", 1),
         ("bv", P), ("bo", P), ("gate", EXPERTS), ("ebias", EXPERTS)]


def columns(names):
    at, where = 0, {}
    for name, n in names:
        where[name] = (at, at + n)
        at += n
    return where, at


SMALL_AT, SMALL_W = columns(SMALL)


def xattn_moe(nc, x_tok, small_in, weights_in, route_rows, out_t):
    ctx = ExitStack()
    with ctx:
        def sb(name, shape, dt=F32):
            return ctx.enter_context(nc.sbuf_tensor(name, shape, dt))

        def sem(name):
            return ctx.enter_context(nc.semaphore(name))

        routes = sb("routes", [P, SPREAD_BY_DMA * T])
        x, xn, xb, att, y = (routes[:, n * T:(n + 1) * T] for n in range(5))
        probs = routes[:, 5 * T:(5 + HG) * T].rearrange("p (b g s) -> p b g s", b=B, g=HG)
        small = sb("small", [P, SMALL_W])
        raw_w = sb("raw_w", [P, (PAIRS + 1) * W_PAIR])

        def part(name):
            return small[:, SMALL_AT[name][0]:SMALL_AT[name][1]]

        eps_col = sb("eps_col", [P, 1])
        act_scratch = sb("act_scratch", [P, 1])
        warm = sb("warm", [P, SEQ], BF16)
        pool_scratch = sb("pool_scratch", [P, 1])
        ident = sb("ident", [P, P])
        ident_bf = sb("ident_bf", [P, P], BF16)
        head_of_row = sb("head_of_row", [P, HEADS])
        local_head = sb("local_head", [P, HPG, HD])
        neg_pick = sb("neg_pick", [HEADS, HG, P])
        neg_pick_r = sb("neg_pick_r", [HEADS, HG, P], F32R)
        pick = sb("pick", [PARTS * EXPERTS, (K + 1) * P], BF16)

        k_hi = sb("k_hi", [P, B * KEYS], F32R)
        k_lo = sb("k_lo", [P, B * KEYS])
        kblk_hi = sb("kblk_hi", [P, B, HEADS, KEYS], F32R)
        kblk_lo = sb("kblk_lo", [P, B, HEADS, KEYS], F32R)
        v_rep = sb("v_rep", [P, B, P])
        v_ext = sb("v_ext", [P, B, HG, VE_W])
        wq_hi = sb("wq_hi", [P, P], F32R)
        wq_lo = sb("wq_lo", [P, P], F32R)
        stats = sb("stats", [P, B * TPB, 6])
        mv = sb("mv", [P, B * TPB, 2])
        std = sb("std", [P, B * TPB])
        rstd = sb("rstd", [P, B * TPB])
        xn_hi = sb("xn_hi", [P, T], F32R)
        xn_lo = sb("xn_lo", [P, T], F32R)
        q_hi = sb("q_hi", [P, T], F32R)
        q_lo = sb("q_lo", [P, T], F32R)
        smax = sb("smax", [P, B * TPB, HEADS])
        smax_t = sb("smax_t", [HEADS, T], F32R)
        rden = sb("rden", [P, B * TPB, HG, HPG])
        att_t = sb("att_t", [P, T])

        stats2 = sb("stats2", [P, B * TPB, 6])
        mv2 = sb("mv2", [P, B * TPB, 2])
        rstd2 = sb("rstd2", [P, B * TPB])
        minus_half = sb("minus_half", [P, TPB])
        var_eps = sb("var_eps", [P, B * TPB])
        yn = sb("yn", [P, T])
        yn_hi = sb("yn_hi", [P, T], F32R)
        yn_lo = sb("yn_lo", [P, T], F32R)
        gate_hi = sb("gate_hi", [P, EXPERTS], F32R)
        gate_lo = sb("gate_lo", [P, EXPERTS], F32R)
        score_t = sb("score_t", [EXPERTS, T])
        sfc = sb("sfc", [P, B, TPB, EXPERTS])
        g_pad = GROUPS + TOP_GROUPS
        e_pad = EXPERTS + 8 - TOP_K
        g_max = sb("g_max", [P, B, TPB, g_pad])
        g_top = sb("g_top", [P, B, TPB, 8])
        g_mark = sb("g_mark", [P, B, TPB, g_pad])
        g_sel = sb("g_sel", [P, B, TPB, GROUPS])
        masked = sb("masked", [P, B, TPB, e_pad])
        e_top = sb("e_top", [P, B, TPB, 8])
        e_mark = sb("e_mark", [P, B, TPB, e_pad])
        chosen = sb("chosen", [P, B, TPB, EXPERTS])
        ch_sum = sb("ch_sum", [P, B, TPB])
        ch_sc = sb("ch_sc", [P, B, TPB])
        ch_rec = sb("ch_rec", [P, B, TPB])
        comb = sb("comb", [P, B, TPB, EXPERTS])
        comb_r1 = sb("comb_r1", [P, B, TPB, EXPERTS])
        comb3 = sb("comb3", [P, B, TPB, PARTS, EXPERTS], BF16)
        comb_t = sb("comb_t", [PARTS * EXPERTS, T], BF16)
        comb_rows = sb("comb_rows", [EXPERTS, T])

        r_hi = [sb(f"r_hi{p}", [P, W_PAIR], F32R) for p in range(K)]
        r_lo = [sb(f"r_lo{p}", [P, W_PAIR], F32R) for p in range(K)]
        w_hi = [sb(f"w_hi{s}", [P, W_PAIR], F32R) for s in range(2)]
        w_lo = [sb(f"w_lo{s}", [P, W_PAIR], F32R) for s in range(2)]
        act_g = [sb(f"act_g{b}", [P, SEQ]) for b in range(B)]
        gu = [sb(f"gu{n}", [P, SEQ]) for n in range(AHEAD)]
        h = [sb(f"h{b}", [P, SEQ]) for b in range(B)]
        h_hi = [sb(f"h_hi{b}", [P, SEQ], F32R) for b in range(B)]
        h_lo = [sb(f"h_lo{b}", [P, SEQ], F32R) for b in range(B)]
        result = att_t

        bank = [ctx.enter_context(nc.psum_tensor(f"bank{i}", [P, SEQ], F32)) for i in range(8)]
        k_ps, v_ps = bank[6], bank[5]

        x_in = [sem(f"x_in{b}") for b in range(B)]
        small_in_s = sem("small_in")
        w_in = [sem(f"w_in{n}") for n in range(len(W_CUTS) - 1)]
        rows_out = sem("rows_out")
        routes_in = [sem(f"routes_in{s}") for s in range(2)]
        out_done = sem("out_done")
        eps_set = sem("eps_set")
        warm_set = sem("warm_set")
        ident_set = sem("ident_set")
        heads_set = sem("heads_set")
        neg_pick_set = sem("neg_pick_set")
        pads_set = sem("pads_set")
        pick_set = sem("pick_set")
        xb_ready = sem("xb_ready")
        pool_step = sem("pool_step")
        kblk_lo_ready = sem("kblk_lo_ready")
        vext_ready = sem("vext_ready")
        h_lo_ready = sem("h_lo_ready")
        rstd_ready = sem("rstd_ready")
        gu_row0_ready = sem("gu_row0_ready")
        std_ready = sem("std_ready")
        smax_t_ready = sem("smax_t_ready")
        r_hi_ready = sem("r_hi_ready")
        k_hi_ready = sem("k_hi_ready")
        table = sem("table")
        xn_hi_ready = sem("xn_hi_ready")
        q_hi_ready = sem("q_hi_ready")
        probs_ready = sem("probs_ready")
        att_t_ready = sem("att_t_ready")
        yn_hi_ready = sem("yn_hi_ready")
        sigmoid_ready = sem("sigmoid_ready")
        comb_t_ready = sem("comb_t_ready")
        comb_rows_ready = sem("comb_rows_ready")
        silu_ready = sem("silu_ready")
        up_read = sem("up_read")
        h_hi_ready = sem("h_hi_ready")
        gu_hi_ready = sem("gu_hi_ready")
        d_hi_ready = sem("d_hi_ready")
        vec_step = sem("vec_step")
        kv_read = sem("kv_read")
        small_hi_ready = sem("small_hi_ready")
        var_ready = sem("var_ready")
        xn_ready = sem("xn_ready")
        xn_lo_ready = sem("xn_lo_ready")
        q_lo_ready = sem("q_lo_ready")
        smax_ready = sem("smax_ready")
        kblk_hi_ready = sem("kblk_hi_ready")
        r_lo_ready = sem("r_lo_ready")
        att_ready = sem("att_ready")
        y_ready = sem("y_ready")
        yn_ready = sem("yn_ready")
        yn_lo_ready = sem("yn_lo_ready")
        comb3_ready = sem("comb3_ready")
        gu_ready = sem("gu_ready")
        h_ready = sem("h_ready")
        gu_lo_ready = sem("gu_lo_ready")
        d_lo_ready = sem("d_lo_ready")
        result_ready = [sem(f"result_ready{b}") for b in range(B)]
        kv_done = sem("kv_done")
        xn_t_done = sem("xn_t_done")
        q_done = sem("q_done")
        score_done = sem("score_done")
        smax_t_done = sem("smax_t_done")
        score_t_done = sem("score_t_done")
        av_done = sem("av_done")
        att_t_done = sem("att_t_done")
        proj_done = sem("proj_done")
        yn_t_done = sem("yn_t_done")
        logits_done = sem("logits_done")
        score_back = sem("score_back")
        comb_t_done = sem("comb_t_done")
        comb_rows_done = sem("comb_rows_done")
        gate_done = sem("gate_done")
        up_done = sem("up_done")
        spread_done = sem("spread_done")
        down_done = sem("down_done")

        def gated_up_to(n):
            return (gu_row0_ready, n + 1) if isinstance(n, int) and n < K else (gu_ready, n - K + 1)

        def routed_up_to(n):
            return None if n in (0, K) else n if n < K else n - 1

        def tile_of(tensor, b, t, w=P):
            i = b * TPB + t
            return tensor[:, i * w:(i + 1) * w]

        def row(tensor, b):
            return tensor[:, b * SEQ:(b + 1) * SEQ]

        def keys_of(keys, b):
            return keys[:, b * KEYS:(b + 1) * KEYS].bitcast(F32).unsqueeze(1).broadcast_to([P, HEADS, KEYS])

        def router_scores(b):
            return bank[6 + b][:, SEQ // 2:SEQ // 2 + TPB * EXPERTS].rearrange("p (t e) -> p t e", t=TPB)

        def head_mask():
            return head_of_row[:].unsqueeze(2).broadcast_to([P, HEADS, KEYS])

        block = ctx.enter_context(nc.Block())

        @block.sync
        def _(sp):
            for b in range(B):
                sp.dma_start(row(x, b), x_tok[:, b * SEQ:(b + 1) * SEQ]).then_inc(x_in[b], 16)
            for n, (lo, hi) in enumerate(zip(W_CUTS, W_CUTS[1:])):
                sp.dma_start(raw_w[:, lo * W_PAIR:hi * W_PAIR],
                             weights_in[:, lo * W_PAIR:hi * W_PAIR]).then_inc(w_in[n], 16)
            sp.wait_ge(comb_rows_ready, B)
            sp.dma_start(route_rows[:, :], comb_rows[:]).then_inc(rows_out, 16)
            sp.wait_ge(rows_out, 16)
            for n in range(SPREAD_BY_DMA):
                if n >= 2:
                    sp.wait_ge(routes_in[n % 2], 2 * 16 * (n // 2))
                for j in range(2):
                    expert = (K + 1 + n) * 2 + j
                    sp.dma_start(routes[j * INTER:(j + 1) * INTER, n * T:(n + 1) * T],
                                 route_rows[expert:expert + 1, :].broadcast_to([INTER, T])
                                 ).then_inc(routes_in[n % 2], 16)
            for b in range(B):
                sp.wait_ge(result_ready[b], 1)
                sp.dma_start(out_t[:, b * SEQ:(b + 1) * SEQ], row(result, b)).then_inc(out_done, 16)
            sp.wait_ge(out_done, 16 * B)

        @block.gpsimd
        def _(pool):
            steps = [0]

            def step(ins):
                steps[0] += 1
                ins.then_inc(pool_step, 1)
                pool.wait_ge(pool_step, steps[0])

            nc.gpsimd.memset(eps_col[:], EPS).then_inc(eps_set, 1)
            nc.gpsimd.memset(warm[:], 0.0).then_inc(warm_set, 1)
            step(nc.gpsimd.memset(ident[:], 0.0))
            nc.gpsimd.affine_select(out=ident[:], in_=ident[:], compare_op=ALU.not_equal, fill=1.0, base=0,
                                    pattern=[[-1, P]], channel_multiplier=1).then_inc(ident_set, 1)
            step(nc.gpsimd.memset(head_of_row[:], 1.0))
            step(nc.gpsimd.affine_select(out=head_of_row[:], in_=head_of_row[:], compare_op=ALU.is_ge, fill=0.0,
                                         base=0, pattern=[[-HD, HEADS]], channel_multiplier=1))
            nc.gpsimd.affine_select(out=head_of_row[:], in_=head_of_row[:], compare_op=ALU.is_ge, fill=0.0,
                                    base=HD - 1, pattern=[[HD, HEADS]], channel_multiplier=-1).then_inc(heads_set, 1)
            step(nc.gpsimd.memset(local_head[:], 1.0))
            step(nc.gpsimd.affine_select(out=local_head[:], in_=local_head[:], compare_op=ALU.is_ge, fill=0.0,
                                         base=0, pattern=[[-KEYS, HPG], [0, HD]], channel_multiplier=1))
            step(nc.gpsimd.affine_select(out=local_head[:], in_=local_head[:], compare_op=ALU.is_ge, fill=0.0,
                                         base=KEYS - 1, pattern=[[KEYS, HPG], [0, HD]], channel_multiplier=-1))
            step(nc.gpsimd.memset(neg_pick[:], -1.0))
            nc.gpsimd.affine_select(out=neg_pick_r[:].rearrange("p g (h k) -> p g h k", h=HPG),
                                    in_=neg_pick[:].rearrange("p g (h k) -> p g h k", h=HPG),
                                    compare_op=ALU.is_equal, fill=0.0, base=0,
                                    pattern=[[-HPG, HG], [-1, HPG], [0, KEYS]],
                                    channel_multiplier=1).then_inc(neg_pick_set, 1)
            pool.wait_ge(heads_set, 1)
            pool.wait_ge(k_hi_ready, 1)
            for b in range(B):
                nc.gpsimd.tensor_tensor(kblk_hi[:, b], keys_of(k_hi, b), head_mask(),
                                        ALU.mult).then_inc(kblk_hi_ready, 1)
            pool.wait_ge(kv_read, 1)
            for b in range(B):
                nc.gpsimd.tensor_tensor(kblk_lo[:, b], keys_of(k_lo, b), head_mask(),
                                        ALU.mult).then_inc(kblk_lo_ready, 1)
            pool.wait_ge(kv_read, 2)
            for b in range(B):
                mask = local_head[:].rearrange("p h d -> p (h d)").unsqueeze(1).broadcast_to([P, HG, HPG * HD])
                nc.gpsimd.tensor_tensor(v_ext[:, b, :, 0:HPG * HD],
                                        v_rep[:, b].rearrange("p (g c) -> p g c", g=HG), mask,
                                        ALU.mult).then_inc(vext_ready, 1)
                nc.gpsimd.tensor_copy(v_ext[:, b, :, HPG * HD:VE_W],
                                      local_head[:, :, 0].unsqueeze(1).broadcast_to([P, HG, HPG])
                                      ).then_inc(vext_ready, 1)
            pool.wait_ge(small_in_s, 16)
            for b in range(B):
                pool.wait_ge(x_in[b], 16)
                nc.gpsimd.tensor_tensor(row(xb, b).rearrange("p (t f) -> p t f", t=TPB),
                                        row(x, b).rearrange("p (t f) -> p t f", t=TPB),
                                        part("bo").unsqueeze(1).broadcast_to([P, TPB, P]),
                                        ALU.add).then_inc(xb_ready, 1)
            nc.gpsimd.memset(g_max[:], SENTINEL).then_inc(pads_set, 1)
            nc.gpsimd.memset(masked[:], SENTINEL).then_inc(pads_set, 1)
            pool.wait_ge(ident_set, 1)
            nc.gpsimd.tensor_copy(ident_bf[:], ident[:]).then_inc(ident_set, 1)
            step(nc.gpsimd.memset(pick[:], 0.0))
            for k in range(PARTS):
                step(nc.gpsimd.affine_select(out=pick[:], in_=pick[:], compare_op=ALU.not_equal, fill=1.0,
                                             base=-k * EXPERTS, pattern=[[-2, K + 1], [-1, 2], [0, INTER]],
                                             channel_multiplier=1))
            nc.gpsimd.memset(pool_scratch[:], 0.0).then_inc(pick_set, 1)

            def low_part(n, j, src=None):
                pool.wait_ge(h_hi_ready, n + 1)
                nc.gpsimd.tensor_tensor(h_lo[j][:], (src or h[j])[:], h_hi[j][:].bitcast(F32),
                                        ALU.subtract).then_inc(h_lo_ready, 1)

            def gated(n):
                pool.wait_ge(silu_ready, n + 1)
                pool.wait_ge(up_read, n + 1)
                nc.gpsimd.tensor_tensor(gu[n][:], gu[n][:], act_g[n % 2][:], ALU.mult).then_inc(gu_row0_ready, 1)

            def deviation(b):
                v = slice(b * TPB, (b + 1) * TPB)
                pool.wait_ge(var_ready, B + b + 1)
                step(nc.gpsimd.tensor_scalar(var_eps[:, v], mv2[:, v, 1], EPS, 0.0, ALU.add, ALU.add))
                nc.gpsimd.tensor_tensor(rstd2[:, v], var_eps[:, v], minus_half[:], ALU.pow).then_inc(rstd_ready, 1)

            step(nc.gpsimd.memset(minus_half[:], -0.5))
            deviation(0)
            gated(0)
            gated(1)
            deviation(1)
            gated(2)
            low_part(0, 0, gu[0])
            gated(3)
            gated(4)
            low_part(1, 1)
            gated(5)
            low_part(2, 0)
            for n in range(3, B * (K + 2)):
                low_part(n, n % 2, gu[n] if n == K else None)
            with pool.Fori(0, LOOPS) as it:
                for u in range(2 * B):
                    low_part(it * (2 * B) + (B * (K + 2) + u), u % 2)

        @block.scalar
        def _(act):
            act.dma_start(small[:], small_in[:, :]).then_inc(small_in_s, 16)

            def deviation(n, m, b):
                act.wait_ge(var_ready, n)
                nc.scalar.activation(std[:, b * TPB:(b + 1) * TPB], m[:, b * TPB:(b + 1) * TPB, 1], ACT.Sqrt,
                                     bias=eps_col[:]).then_inc(std_ready, 1)

            def evacuate(dst, src, wait, n, ready):
                act.wait_ge(wait, n)
                nc.scalar.activation(dst, src, ACT.Copy).then_inc(ready, 1)

            def query(b):
                act.wait_ge(q_done, b + 1)
                nc.scalar.activation(row(q_hi, b), bank[2 + b][:], ACT.Identity,
                                     bias=part("bq")).then_inc(q_hi_ready, 1)

            def exps(b, g):
                act.wait_ge(score_t_done, b * HG + g + 1)
                nc.scalar.activation(probs[:, b, g], bank[4 + g % 2][:], ACT.Exp,
                                     scale=HD ** -0.5).then_inc(probs_ready, 1)

            def sigmoid(b):
                act.wait_ge(logits_done, b + 1)
                nc.scalar.activation(score_t[:, b * SEQ:(b + 1) * SEQ], bank[6 + b][0:EXPERTS, :],
                                     ACT.Sigmoid).then_inc(sigmoid_ready, 1)

            tables = [0]

            def load_table(func):
                if tables[0]:
                    act.wait_ge(table, tables[0])
                tables[0] += 1
                nc.scalar.activation(act_scratch[:], eps_col[:], func).then_inc(table, 1)

            def weights_high(dst, pair, at, n, ready):
                nc.scalar.activation(dst, raw_w[:, bass.ds(pair * W_PAIR + at, n)], ACT.Copy).then_inc(ready, 1)

            def resident_high(pair):
                if pair in W_CUTS:
                    act.wait_ge(w_in[W_CUTS.index(pair)], 16)
                weights_high(r_hi[pair][:], pair, 0, W_PAIR, r_hi_ready)

            def silu(n, b, j, first=False):
                act.wait_ge(gate_done, n + 1)
                if not first:
                    act.wait_ge(*gated_up_to(n - 2))
                nc.scalar.activation(act_g[j][:], bank[2 + b][:], ACT.Silu).then_inc(silu_ready, 1)

            def up_out(n):
                act.wait_ge(up_done, n + 1)
                nc.scalar.activation(gu[n][:], bank[4 + n % 2][:], ACT.Copy).then_inc(up_read, 1)

            def high_part(n, j, first=False, weighted=None):
                if weighted is None:
                    act.wait_ge(*gated_up_to(n))
                else:
                    act.wait_ge(h_ready, weighted)
                if not first:
                    act.wait_ge(down_done, n - 1)
                src = gu[n] if weighted is None else h[j]
                nc.scalar.activation(h_hi[j][:], src[:], ACT.Copy).then_inc(h_hi_ready, 1)

            def split_high(n):
                high_part(n, n % 2, first=n < 2, weighted=routed_up_to(n))

            act.wait_ge(eps_set, 1)
            load_table(ACT.Sqrt)
            deviation(1, mv, 0)
            act.wait_ge(kv_done, 1)
            nc.scalar.activation(k_hi[:], k_ps[:, 0:B * KEYS], ACT.Identity, bias=part("bk")).then_inc(k_hi_ready, 1)
            evacuate(row(xn_hi, 0), bank[0][:], xn_t_done, 1, xn_hi_ready)
            deviation(2, mv, 1)
            query(0)
            load_table(ACT.Exp)
            evacuate(row(xn_hi, 1), bank[1][:], xn_t_done, 2, xn_hi_ready)
            resident_high(0)
            evacuate(row(smax_t, 0), bank[0][0:HEADS, :], smax_t_done, 1, smax_t_ready)
            query(1)
            for g in range(HG):
                exps(0, g)
            resident_high(1)
            resident_high(2)
            evacuate(row(smax_t, 1), bank[1][0:HEADS, :], smax_t_done, 2, smax_t_ready)
            exps(1, 0)
            evacuate(row(att_t, 0), bank[2][:], att_t_done, 1, att_t_ready)
            resident_high(3)
            exps(1, 1)
            exps(1, 2)
            exps(1, 3)
            load_table(ACT.Sigmoid)
            resident_high(4)
            resident_high(5)
            evacuate(row(yn_hi, 0), bank[2][:], yn_t_done, 1, yn_hi_ready)
            sigmoid(0)
            load_table(ACT.Silu)
            silu(0, 0, 0, first=True)
            evacuate(row(att_t, 1), bank[3][:], att_t_done, 2, att_t_ready)
            up_out(0)
            silu(1, 0, 1, first=True)
            up_out(1)
            silu(2, 0, 0)
            up_out(2)
            split_high(0)
            silu(3, 0, 1)
            up_out(3)
            silu(4, 0, 0)
            evacuate(row(yn_hi, 1), bank[3][:], yn_t_done, 2, yn_hi_ready)
            evacuate(row(comb_t, 0), bank[6][:].bitcast(BF16)[0:PARTS * EXPERTS, 0:SEQ],
                     comb_t_done, 1, comb_t_ready)
            up_out(4)
            load_table(ACT.Sigmoid)
            sigmoid(1)
            up_out(5)
            split_high(1)
            load_table(ACT.Silu)
            silu(5, 0, 1)
            for n in range(K, AHEAD):
                silu(n, 1, n % 2)
                if n == AHEAD - 2:
                    act.wait_ge(w_in[W_CUTS.index(K)], 16)
                    weights_high(w_hi[K % 2][:, 0:W_GU], K, 0, W_GU, gu_hi_ready)
                    evacuate(row(comb_t, 1), bank[7][:].bitcast(BF16)[0:PARTS * EXPERTS, 0:SEQ],
                             comb_t_done, 2, comb_t_ready)
                split_high(n - K + 2)
                if n == AHEAD - 2:
                    for b in range(B):
                        evacuate(row(comb_rows, b), bank[(4, 2)[b]][0:EXPERTS, :], comb_rows_done, b + 1,
                                 comb_rows_ready)
            for arrived in w_in[W_CUTS.index(K) + 1:]:
                act.wait_ge(arrived, 16)
            for n in range(AHEAD, AHEAD + 2 * B):
                pair, b = n // B, n % B
                if b == 0:
                    if pair > K:
                        act.wait_ge(up_done, n)
                    weights_high(w_hi[1 - pair % 2][:, 0:W_GU], pair + 1, 0, W_GU, gu_hi_ready)
                split_high(SPREAD_BEHIND[n - AHEAD][0] - 1)
                silu(n, b, b)
                if n < AHEAD + 3:
                    split_high(SPREAD_BEHIND[n - AHEAD][0])
                if b == 1:
                    weights_high(w_hi[pair % 2][:, W_GU:W_PAIR], pair, W_GU, W_D, d_hi_ready)

            def pair_steps(pair, slot, last=False):
                n = pair * B
                if not last:
                    act.wait_ge(up_done, n)
                    weights_high(w_hi[1 - slot][:, 0:W_GU], pair + 1, 0, W_GU, gu_hi_ready)
                silu(n, 0, 0)
                act.wait_ge(h_ready, n - 2)
                nc.scalar.activation(h_hi[1][:], h[1][:], ACT.Copy).then_inc(h_hi_ready, 1)
                silu(n + 1, 1, 1)
                if not last:
                    weights_high(w_hi[slot][:, W_GU:W_PAIR], pair, W_GU, W_D, d_hi_ready)
                    high_part(n, 0, weighted=n - 1)

            with act.Fori(0, LOOPS) as it:
                for s in range(2):
                    pair_steps(it * 2 + (K + 2 + s), (K + 2 + s) % 2)
            pair_steps(PAIRS, PAIRS % 2, last=True)
            act.wait_ge(down_done, UNITS)
            nc.scalar.activation(row(result, 1), bank[1][:], ACT.Copy).then_inc(result_ready[1], 1)

        @block.vector
        def _(dve):
            steps = [0]

            def mark(ins):
                steps[0] += 1
                ins.then_inc(vec_step, 1)

            def settle():
                dve.wait_ge(vec_step, steps[0])

            def step(ins):
                mark(ins)
                settle()

            def moments(src, st, out, b):
                for t in range(TPB):
                    mark(nc.vector.bn_stats(st[:, b * TPB + t], tile_of(src, b, t)))
                settle()
                for t in range(TPB):
                    last = nc.vector.bn_aggr(out[:, b * TPB + t], st[:, b * TPB + t])
                last.then_inc(var_ready, 1)

            def scaled(src, m, r, out, b, ready):
                for t in range(TPB):
                    i = b * TPB + t
                    nc.vector.tensor_scalar(tile_of(out, b, t), tile_of(src, b, t), m[:, i, 0:1], r[:, i:i + 1],
                                            ALU.subtract, ALU.mult).then_inc(ready, 1)

            def normalise(src, m, r, out, b, n, ready):
                v = slice(b * TPB, (b + 1) * TPB)
                dve.wait_ge(std_ready, n)
                step(nc.vector.reciprocal(r[:, v], std[:, v]))
                scaled(src, m, r, out, b, ready)

            def normalise_again(b):
                dve.wait_ge(rstd_ready, b + 1)
                scaled(y, mv2, rstd2, yn, b, yn_ready)

            def low_of(lo, hi, src, b, hi_ready, ready):
                dve.wait_ge(hi_ready, b + 1)
                nc.vector.tensor_tensor(row(lo, b), src[:], row(hi, b).bitcast(F32), ALU.subtract).then_inc(ready, 1)

            def query_low(b):
                dve.wait_ge(q_hi_ready, b + 1)
                nc.vector.scalar_tensor_tensor(row(q_lo, b), bank[2 + b][:], part("bq"), row(q_hi, b).bitcast(F32),
                                               ALU.add, ALU.subtract).then_inc(q_lo_ready, 1)

            def score_max(b, t):
                i = b * TPB + t
                dve.wait_ge(score_done, i + 1)
                nc.vector.tensor_reduce(out=smax[:, i], in_=bank[6 + t % 2][:].rearrange("p (h k) -> p h k", k=KEYS),
                                        op=ALU.max, axis=AXIS_X).then_inc(smax_ready, 1)

            def attended(b, half):
                where = bank[b] if half else bank[2 + b]
                i = b * TPB + 2 * half
                dve.wait_ge(av_done, b * TPB // 2 + half + 1)
                sums = where[:, 0:2 * HG * VE_W].rearrange("p (g c) -> p g c", c=VE_W)
                dens = rden[:, i:i + 2].rearrange("p t g h -> p (t g) h")
                step(nc.vector.reciprocal(dens, sums[:, :, HPG * HD:VE_W]))
                nc.vector.tensor_tensor(
                    att[:, i * P:(i + 2) * P].rearrange("p (g h d) -> p g h d", h=HPG, d=HD),
                    sums[:, :, 0:HPG * HD].rearrange("p g (h d) -> p g h d", d=HD),
                    dens.unsqueeze(3).broadcast_to([P, 2 * HG, HPG, HD]), ALU.mult).then_inc(att_ready, 1)

            def residual(b):
                dve.wait_ge(proj_done, b + 1)
                dve.wait_ge(xb_ready, b + 1)
                nc.vector.tensor_tensor(row(y, b), bank[b][:], row(xb, b), ALU.add).then_inc(y_ready, 1)
                dve.wait_ge(y_ready, b + 1)
                moments(y, stats2, mv2, b)

            def route_groups(b):
                dve.wait_ge(score_back, b + 1)
                step(nc.vector.tensor_tensor(sfc[:, b], router_scores(b),
                                             part("ebias").unsqueeze(1).broadcast_to([P, TPB, EXPERTS]), ALU.add))
                step(nc.vector.tensor_reduce(out=g_max[:, b, :, 0:GROUPS],
                                             in_=sfc[:, b].rearrange("p t (g e) -> p t g e", e=EPG),
                                             op=ALU.max, axis=AXIS_X))
                for t in range(TPB):
                    mark(nc.vector.max(g_top[:, b, t], g_max[:, b, t, 0:GROUPS]))
                settle()
                step(nc.vector.memset(g_top[:, b, :, TOP_GROUPS:8], SENTINEL))
                for t in range(TPB):
                    mark(nc.vector.match_replace(out=g_mark[:, b, t], in_to_replace=g_top[:, b, t],
                                                 in_values=g_max[:, b, t], imm_value=TAKEN))

            def route_experts(b):
                settle()
                step(nc.vector.tensor_scalar(g_sel[:, b], g_mark[:, b, :, 0:GROUPS], TAKEN, None, ALU.is_equal))
                step(nc.vector.tensor_tensor(
                    masked[:, b, :, 0:EXPERTS].rearrange("p t (g e) -> p t g e", e=EPG),
                    sfc[:, b].rearrange("p t (g e) -> p t g e", e=EPG),
                    g_sel[:, b].unsqueeze(3).broadcast_to([P, TPB, GROUPS, EPG]), ALU.mult))
                for t in range(TPB):
                    mark(nc.vector.max(e_top[:, b, t], masked[:, b, t, 0:EXPERTS]))
                settle()
                step(nc.vector.memset(e_top[:, b, :, TOP_K:8], SENTINEL))
                for t in range(TPB):
                    mark(nc.vector.match_replace(out=e_mark[:, b, t], in_to_replace=e_top[:, b, t],
                                                 in_values=masked[:, b, t], imm_value=TAKEN))

            def route_weights(b):
                settle()
                step(nc.vector.scalar_tensor_tensor(chosen[:, b], e_mark[:, b, :, 0:EXPERTS], TAKEN, router_scores(b),
                                                    ALU.is_equal, ALU.mult))
                step(nc.vector.tensor_reduce(out=ch_sum[:, b], in_=chosen[:, b], op=ALU.add, axis=AXIS_X))
                step(nc.vector.tensor_scalar(ch_sc[:, b], ch_sum[:, b], 1e-20, 1.0 / ROUTE_SCALE, ALU.add, ALU.mult))
                step(nc.vector.reciprocal(ch_rec[:, b], ch_sc[:, b]))
                mark(nc.vector.tensor_tensor(comb[:, b], chosen[:, b],
                                             ch_rec[:, b].unsqueeze(2).broadcast_to([P, TPB, EXPERTS]), ALU.mult))

            def route_parts(b):
                settle()
                step(nc.vector.tensor_copy(comb3[:, b, :, 0], comb[:, b]))
                step(nc.vector.tensor_tensor(comb_r1[:, b], comb[:, b], comb3[:, b, :, 0], ALU.subtract))
                step(nc.vector.tensor_copy(comb3[:, b, :, 1], comb_r1[:, b]))
                nc.vector.tensor_tensor(comb3[:, b, :, 2], comb_r1[:, b], comb3[:, b, :, 1],
                                        ALU.subtract).then_inc(comb3_ready, 1)

            def weights_low(dst, hi, pair, at, n, hi_ready, count, ready):
                dve.wait_ge(hi_ready, count)
                nc.vector.tensor_tensor(dst, raw_w[:, bass.ds(pair * W_PAIR + at, n)], hi.bitcast(F32),
                                        ALU.subtract).then_inc(ready, 1)

            def resident_low(pair):
                if pair in W_CUTS:
                    dve.wait_ge(w_in[W_CUTS.index(pair)], 16)
                weights_low(r_lo[pair][:], r_hi[pair][:], pair, 0, W_PAIR, r_hi_ready, pair + 1, r_lo_ready)

            def gated(n, b, j, at, free=None, count=0):
                dve.wait_ge(silu_ready, n + 1)
                dve.wait_ge(up_done, n + 1)
                if free is not None:
                    dve.wait_ge(free, count)
                nc.vector.tensor_tensor(gu[at][:], bank[4 + b][:], act_g[j][:], ALU.mult).then_inc(gu_ready, 1)

            def gated_ahead(n):
                gated(n, 0 if n < K else 1, n % 2, n)

            def weighted(n, b, j, at, routed, first=False):
                dve.wait_ge(spread_done, routed)
                dve.wait_ge(*gated_up_to(n))
                weigh(n, j, at, bank[6 + b][:], first)

            def weighted_late(n, b, pair, routes_sem, count):
                dve.wait_ge(routes_sem, count)
                dve.wait_ge(*gated_up_to(n))
                weigh(n, b, b, routes[:, bass.ds((pair - (K + 2)) * T + b * SEQ, SEQ)])

            def weigh(n, j, at, route, first=False):
                if not first:
                    dve.wait_ge(h_lo_ready, n - 1)
                nc.vector.tensor_tensor(h[j][:], route, gu[at][:], ALU.mult).then_inc(h_ready, 1)

            def down_low(pair, slot):
                weights_low(w_lo[slot][:, W_GU:W_PAIR], w_hi[slot][:, W_GU:W_PAIR], pair, W_GU, W_D,
                            d_hi_ready, pair - K + 1, d_lo_ready)

            def weighted_early(n):
                if n < AHEAD:
                    weighted(n, 0 if n < K else 1, n % 2, n, routed_up_to(n), first=n < 2)
                else:
                    weighted(n, n % B, n % 2, n - AHEAD, routed_up_to(n))

            dve.wait_ge(x_in[0], 16)
            moments(x, stats, mv, 0)
            dve.wait_ge(small_in_s, 16)
            mark(nc.vector.tensor_copy(wq_hi[:], part("wq")))
            mark(nc.vector.tensor_copy(gate_hi[:], part("gate")))
            normalise(x, mv, rstd, xn, 0, 1, xn_ready)
            nc.vector.tensor_tensor(wq_lo[:], part("wq"), wq_hi[:].bitcast(F32), ALU.subtract).then_inc(small_hi_ready, 1)
            dve.wait_ge(x_in[1], 16)
            moments(x, stats, mv, 1)
            low_of(xn_lo, xn_hi, bank[0], 0, xn_hi_ready, xn_lo_ready)
            dve.wait_ge(k_hi_ready, 1)
            nc.vector.scalar_tensor_tensor(k_lo[:], k_ps[:, 0:B * KEYS], part("bk"), k_hi[:].bitcast(F32),
                                           ALU.add, ALU.subtract).then_inc(kv_read, 1)
            dve.wait_ge(kv_done, 2)
            nc.vector.tensor_tensor(v_rep[:], v_ps[:, 0:B * P].rearrange("p (b f) -> p b f", b=B),
                                    part("bv").unsqueeze(1).broadcast_to([P, B, P]), ALU.add).then_inc(kv_read, 1)
            normalise(x, mv, rstd, xn, 1, 2, xn_ready)
            for t in range(TPB):
                score_max(0, t)
            low_of(xn_lo, xn_hi, bank[1], 1, xn_hi_ready, xn_lo_ready)
            query_low(0)
            nc.vector.tensor_tensor(gate_lo[:], part("gate"), gate_hi[:].bitcast(F32),
                                    ALU.subtract).then_inc(small_hi_ready, 1)
            resident_low(0)
            score_max(1, 0)
            score_max(1, 1)
            query_low(1)
            score_max(1, 2)
            score_max(1, 3)
            resident_low(1)
            attended(0, 0)
            resident_low(2)
            attended(0, 1)
            residual(0)
            resident_low(3)
            normalise_again(0)
            attended(1, 0)
            low_of(yn_lo, yn_hi, bank[2], 0, yn_hi_ready, yn_lo_ready)
            resident_low(4)
            resident_low(5)
            attended(1, 1)
            dve.wait_ge(pads_set, 2)
            route_groups(0)
            route_experts(0)
            residual(1)
            route_weights(0)
            normalise_again(1)
            route_parts(0)
            low_of(yn_lo, yn_hi, bank[3], 1, yn_hi_ready, yn_lo_ready)
            weighted_early(1)
            route_groups(1)
            weighted_early(2)
            gated_ahead(6)
            weighted_early(3)
            route_experts(1)
            gated_ahead(7)
            weighted_early(4)
            route_weights(1)
            gated_ahead(8)
            weighted_early(5)
            gated_ahead(9)
            route_parts(1)
            dve.wait_ge(w_in[W_CUTS.index(K)], 16)
            weights_low(w_lo[K % 2][:, 0:W_GU], w_hi[K % 2][:, 0:W_GU], K, 0, W_GU, gu_hi_ready, 1, gu_lo_ready)
            gated_ahead(10)
            weighted_early(7)
            gated_ahead(11)
            weighted_early(8)
            for arrived in w_in[W_CUTS.index(K) + 1:]:
                dve.wait_ge(arrived, 16)
            for n in range(AHEAD, AHEAD + 2 * B):
                pair, b = n // B, n % B
                if b == 0:
                    weights_low(w_lo[1 - pair % 2][:, 0:W_GU], w_hi[1 - pair % 2][:, 0:W_GU], pair + 1, 0, W_GU,
                                gu_hi_ready, pair - K + 2, gu_lo_ready)
                early = [m for m in SPREAD_BEHIND[n - AHEAD][:1] if m < n]
                for m in early:
                    weighted_early(m)
                if n == AHEAD:
                    gated(n, b, b, 0, h_lo_ready, 1)
                else:
                    gated(n, b, b, n - AHEAD, h_ready, n - AHEAD)
                if b == 1:
                    down_low(pair, pair % 2)
                for m in SPREAD_BEHIND[n - AHEAD][len(early):]:
                    weighted_early(m)

            def pair_steps(pair, slot, arrived, last=False):
                n = pair * B
                if not last:
                    weights_low(w_lo[1 - slot][:, 0:W_GU], w_hi[1 - slot][:, 0:W_GU], pair + 1, 0, W_GU,
                                gu_hi_ready, pair - K + 2, gu_lo_ready)
                gated(n, 0, 0, 0, h_ready, n - 3)
                weighted_late(n, 0, pair, routes_in[slot], arrived)
                gated(n + 1, 1, 1, 1, h_ready, n - 2)
                if not last:
                    down_low(pair, slot)
                weighted_late(n + 1, 1, pair, routes_in[slot], arrived)

            with dve.Fori(0, LOOPS) as it:
                for s in range(2):
                    pair_steps(it * 2 + (K + 2 + s), (K + 2 + s) % 2, it * (2 * 16) + 2 * 16)
            pair_steps(PAIRS, PAIRS % 2, 2 * 16 * (LOOPS + 1), last=True)
            dve.wait_ge(down_done, UNITS - 1)
            nc.vector.tensor_copy(row(result, 0), bank[0][:]).then_inc(result_ready[0], 1)

        @block.tensor
        def _(pe):
            def wide(out, lhs_t, rhs, low=None, start=True, stop=True):
                nc.tensor.matmul(out, lhs_t[0], rhs[0], start=start, stop=False)
                nc.tensor.matmul(out, lhs_t[1], rhs[0], start=False, stop=False)
                if low:
                    pe.wait_ge(*low)
                return nc.tensor.matmul(out, lhs_t[0], rhs[1], start=False, stop=stop)

            def turn_tiles(where, src, b, ready, count, done, per_tile=0):
                for t in range(TPB):
                    if per_tile or t == 0:
                        pe.wait_ge(ready, count + per_tile * t)
                    last = nc.tensor.transpose(where[:, t * P:(t + 1) * P], tile_of(src, b, t), ident[:])
                last.then_inc(done, 1)

            def query(b):
                pe.wait_ge(xn_hi_ready, b + 1)
                wide(bank[2 + b][:], (wq_hi[:], wq_lo[:]), (row(xn_hi, b), row(xn_lo, b)),
                     low=(xn_lo_ready, b + 1)).then_inc(q_done, 1)

            def scores(b, t):
                i = b * TPB + t
                if t == 0:
                    pe.wait_ge(q_hi_ready, b + 1)
                    pe.wait_ge(kblk_hi_ready, b + 1)
                if i == 0:
                    pe.wait_ge(kv_read, 2)
                if i >= 2:
                    pe.wait_ge(smax_ready, i - 1)
                nc.tensor.matmul(bank[6 + t % 2][:], tile_of(q_hi, b, t), kblk_hi[:, b].rearrange("p h k -> p (h k)"),
                                 start=True, stop=True).then_inc(score_done, 1)

            def turn_max(b):
                pe.wait_ge(xn_lo_ready, b + 1)
                for t in range(TPB):
                    i = b * TPB + t
                    pe.wait_ge(smax_ready, i + 1)
                    last = nc.tensor.transpose(bank[b][0:HEADS, t * P:(t + 1) * P], smax[:, i], ident[:])
                last.then_inc(smax_t_done, 1)

            def shifted_scores(b, g):
                if g == 0:
                    pe.wait_ge(kblk_lo_ready, b + 1)
                if b * HG + g >= 2:
                    pe.wait_ge(probs_ready, b * HG + g - 1)
                hs = slice(g * HPG, (g + 1) * HPG)
                k_h = kblk_hi[:, b, hs].rearrange("p h k -> p (h k)")
                k_l = kblk_lo[:, b, hs].rearrange("p h k -> p (h k)")
                wide(bank[4 + g % 2][:], (k_h, k_l), (row(q_hi, b), row(q_lo, b)),
                     low=(q_lo_ready, b + 1) if g == 0 else None, stop=False)
                if g == 0:
                    pe.wait_ge(smax_t_ready, b + 1)
                nc.tensor.matmul(bank[4 + g % 2][:], neg_pick_r[:, g], row(smax_t, b),
                                 start=False, stop=True).then_inc(score_t_done, 1)

            def head_sums(b, tiles):
                if tiles[0] == 0:
                    pe.wait_ge(vext_ready, 2 * (b + 1))
                for g in range(HG):
                    if tiles[0] == 0:
                        pe.wait_ge(probs_ready, b * HG + g + 1)
                    for t in tiles:
                        at = (t % 2 * HG + g) * VE_W
                        last = nc.tensor.matmul((bank[2 + b] if t < 2 else bank[b])[:, at:at + VE_W],
                                                probs[:, b, g, t * P:(t + 1) * P], v_ext[:, b, g],
                                                start=True, stop=True)
                if t % 2:
                    last.then_inc(av_done, 1)

            def project(b):
                pe.wait_ge(att_t_ready, b + 1)
                for t in range(TPB):
                    last = nc.tensor.matmul(bank[b][:, t * P:(t + 1) * P], tile_of(att_t, b, t), part("wo"),
                                            start=True, stop=True)
                last.then_inc(proj_done, 1)

            def logits(b):
                pe.wait_ge(yn_hi_ready, b + 1)
                wide(bank[6 + b][0:EXPERTS, :], (gate_hi[:], gate_lo[:]), (row(yn_hi, b), row(yn_lo, b)),
                     low=(yn_lo_ready, b + 1)).then_inc(logits_done, 1)

            def turn_scores(b):
                pe.wait_ge(sigmoid_ready, b + 1)
                for t in range(TPB):
                    last = nc.tensor.transpose(router_scores(b)[:, t], tile_of(score_t, b, t), ident[0:EXPERTS, 0:EXPERTS])
                last.then_inc(score_back, 1)

            def turn_weights(b):
                pe.wait_ge(comb3_ready, b + 1)
                for t in range(TPB):
                    last = nc.tensor.transpose(
                        bank[6 + b][:].bitcast(BF16)[0:PARTS * EXPERTS, t * P:(t + 1) * P],
                        comb3[:, b, t].rearrange("p k e -> p (k e)"), ident_bf[:])
                last.then_inc(comb_t_done, 1)

            def turn_rows(b):
                where = bank[(4, 2)[b]]
                for t in range(TPB):
                    last = nc.tensor.transpose(where[0:EXPERTS, t * P:(t + 1) * P], comb[:, b, t], ident[:])
                last.then_inc(comb_rows_done, 1)

            def gate(b, hi, lo):
                w = slice(0, P)
                wide(bank[2 + b][:], (hi[:, w], lo[:, w]), (row(yn_hi, b), row(yn_lo, b))).then_inc(gate_done, 1)

            def up(b, hi, lo, where):
                w = slice(P, 2 * P)
                wide(where[:], (hi[:, w], lo[:, w]), (row(yn_hi, b), row(yn_lo, b))).then_inc(up_done, 1)

            def gate_up_ahead(n):
                b, hi, lo = n // K, r_hi[n % K], r_lo[n % K]
                if n < K:
                    pe.wait_ge(r_lo_ready, n + 1)
                if n % K:
                    pe.wait_ge(silu_ready, n)
                gate(b, hi, lo)
                if n > K:
                    pe.wait_ge(gu_ready, n - K)
                elif n >= 2:
                    pe.wait_ge(up_read, n - 1 if n < K else K)
                up(b, hi, lo, bank[4 + n % 2 if n < K else 5])

            def spread(b, pair, before=None):
                if before is not None:
                    pe.wait_ge(h_ready, before)
                nc.tensor.matmul(bank[6 + b][:], pick[:, bass.ds((pair - 1) * P, P)], row(comb_t, b),
                                 start=True, stop=True).then_inc(spread_done, 1)

            def spread_early(n):
                if n < AHEAD:
                    before = n - 1 if n % K > 1 else None
                    spread(n // K, n % K, routed_up_to(before) if before else None)
                else:
                    before = n - B if n >= AHEAD + B else (K - 1, AHEAD - 1)[n % B]
                    spread(n % B, n // B, routed_up_to(before))

            def down_early(n):
                if n < AHEAD:
                    down(n, n // K, n % 2, r_hi[n % K], r_lo[n % K])
                else:
                    down(n, n % B, n % 2, w_hi[n // B % 2], w_lo[n // B % 2])

            def inject(b):
                pe.wait_ge(y_ready, b + 1)
                for t in range(TPB):
                    nc.tensor.matmul(bank[b][:, t * P:(t + 1) * P], tile_of(y, b, t), ident[:],
                                     start=t == 0, stop=False)

            def down(n, b, j, hi, lo):
                w = slice(W_GU, W_PAIR)
                pe.wait_ge(h_hi_ready, n + 1)
                wide(bank[b][:], (hi[:, w], lo[:, w]), (h_hi[j][:], h_lo[j][:]),
                     low=(h_lo_ready, n + 1), start=False, stop=False).then_inc(down_done, 1)

            def keep_warm(where, n):
                for _ in range(n):
                    nc.tensor.matmul(where[:], warm[:, 0:P], warm[:], start=True, stop=True)

            pe.wait_ge(warm_set, 1)
            keep_warm(bank[7], WARM)
            pe.wait_ge(small_in_s, 16)
            ctx_t = part("ctx4T").rearrange("p (b r k) -> p b r k", b=B, r=HPG)
            nc.tensor.matmul(k_ps[:, 0:B * KEYS], part("wk"), ctx_t[:, :, 0, :],
                             start=True, stop=True).then_inc(kv_done, 1)
            pe.wait_ge(ident_set, 1)
            turn_tiles(bank[0], xn, 0, xn_ready, 1, xn_t_done, per_tile=1)
            for b in range(B):
                last = nc.tensor.matmul(v_ps[:, b * P:(b + 1) * P], part("ctx4T")[:, b * P:(b + 1) * P],
                                        part("wv"), start=True, stop=True)
            last.then_inc(kv_done, 1)
            pe.wait_ge(small_hi_ready, 1)
            query(0)
            keep_warm(bank[4], 2)
            scores(0, 0)
            scores(0, 1)
            turn_tiles(bank[1], xn, 1, xn_ready, TPB + 1, xn_t_done, per_tile=1)
            scores(0, 2)
            scores(0, 3)
            keep_warm(bank[4], 2)
            turn_max(0)
            query(1)
            pe.wait_ge(neg_pick_set, 1)
            for g in range(HG):
                shifted_scores(0, g)
                scores(1, g)
            head_sums(0, (0, 1))
            turn_max(1)
            head_sums(0, (2, 3))
            shifted_scores(1, 0)
            turn_tiles(bank[2], att, 0, att_ready, 2, att_t_done)
            shifted_scores(1, 1)
            project(0)
            shifted_scores(1, 2)
            shifted_scores(1, 3)
            inject(0)
            head_sums(1, (0,))
            head_sums(1, (1,))
            turn_tiles(bank[2], yn, 0, yn_ready, 1, yn_t_done, per_tile=1)
            head_sums(1, (2,))
            pe.wait_ge(small_hi_ready, 2)
            logits(0)
            head_sums(1, (3,))
            turn_scores(0)
            gate_up_ahead(0)
            turn_tiles(bank[3], att, 1, att_ready, 3 + 1, att_t_done)
            gate_up_ahead(1)
            project(1)
            gate_up_ahead(2)
            inject(1)
            gate_up_ahead(3)
            gate_up_ahead(4)
            turn_tiles(bank[3], yn, 1, yn_ready, 2 * TPB, yn_t_done)
            pe.wait_ge(ident_set, 2)
            turn_weights(0)
            gate_up_ahead(5)
            logits(1)
            pe.wait_ge(pick_set, 1)
            pe.wait_ge(comb_t_ready, 1)
            spread_early(1)
            down_early(0)
            turn_scores(1)
            for n in range(K, AHEAD):
                if n - K + 2 < K:
                    spread_early(n - K + 2)
                gate_up_ahead(n)
                if n == AHEAD - 2:
                    turn_weights(1)
                    for b in range(B):
                        turn_rows(b)
                down_early(n - K + 1)
                if n == AHEAD - 2:
                    pe.wait_ge(comb_t_ready, 2)
                if n >= AHEAD - 2:
                    spread_early(n - 3)
            for n in range(AHEAD, AHEAD + 2 * B):
                pair, b = n // B, n % B
                if b == 0:
                    pe.wait_ge(gu_lo_ready, pair - K + 1)
                before = n - B if n >= AHEAD + B else (K - 1, AHEAD - 1)[b]
                first, *second = SPREAD_BEHIND[n - AHEAD]
                if n == AHEAD:
                    pe.wait_ge(comb_rows_ready, B)
                pe.wait_ge(silu_ready, before + 1)
                gate(b, w_hi[pair % 2], w_lo[pair % 2])
                spread_early(first)
                if first >= AHEAD + 2:
                    pe.wait_ge(d_lo_ready, 1)
                down_early(first - 2)
                if before < K:
                    pe.wait_ge(up_read, K)
                else:
                    pe.wait_ge(gu_ready, before - K + 1)
                up(b, w_hi[pair % 2], w_lo[pair % 2], bank[4 + b])
                for m in second:
                    spread_early(m)
                    if m == AHEAD + 2:
                        pe.wait_ge(d_lo_ready, 1)
                    down_early(m - 2)

            def down_before(pair, slot, b):
                if b == 0:
                    pe.wait_ge(d_lo_ready, pair - K)
                down(pair * B + b - 2, b, b, w_hi[1 - slot], w_lo[1 - slot])

            def pair_steps(pair, slot, last=False):
                pe.wait_ge(gu_lo_ready, pair - K + 1)
                for b in range(B):
                    n = pair * B + b
                    pe.wait_ge(silu_ready, n - 1)
                    gate(b, w_hi[slot], w_lo[slot])
                    pe.wait_ge(gu_ready, n - 1 - K)
                    up(b, w_hi[slot], w_lo[slot], bank[4 + b])
                    if not last:
                        down_before(pair, slot, b)
                if last:
                    for b in range(B):
                        down_before(pair, slot, b)

            with pe.Fori(0, LOOPS) as it:
                for s in range(2):
                    pair_steps(it * 2 + (K + 2 + s), (K + 2 + s) % 2)
            pair_steps(PAIRS, PAIRS % 2, last=True)
            for b in range(B):
                pe.wait_ge(h_ready, UNITS - 1 - B + b)
                nc.tensor.matmul(bank[b][:], raw_w[:, PAIRS * W_PAIR + W_GU:(PAIRS + 1) * W_PAIR], h[b][:],
                                 start=False, stop=True).then_inc(down_done, 1)


def kernel(**inputs):
    import numpy as _np
    import concourse.bacc as _bacc
    from concourse import mybir as _mybir
    from concourse.bass_utils import run_bass_kernel_spmd as _run

    a = {k.removeprefix("L0_"): _np.asarray(v) for k, v in inputs.items()}
    x_tok = a["x"].reshape(B * TPB, P, P).transpose(1, 0, 2).reshape(P, T)
    ctx_t = a["ctx_1024"].transpose(2, 0, 1)
    over = lambda v: _np.broadcast_to(v[None, :], (P, v.shape[0]))
    small = {
        "ctx4T": _np.broadcast_to(ctx_t[:, :, None, :], (P, B, HPG, KEYS)).reshape(P, B * P),
        "wk": a["xattn_Wk"], "wv": a["xattn_Wv"], "wq": a["xattn_Wq"], "wo": a["xattn_Wo"],
        "bq": a["xattn_bq"][:, None], "bk": a["xattn_bk"][:, None],
        "bv": over(a["xattn_bv"]), "bo": over(a["xattn_bo"]),
        "gate": a["ffn_gate_weight"].T, "ebias": over(a["ffn_e_score_correction_bias"]),
    }
    gu = a["ffn_experts_gate_up"].reshape(PAIRS, 2, 2, INTER, P).transpose(4, 0, 2, 1, 3).reshape(P, PAIRS, W_GU)
    down = a["ffn_experts_down"].transpose(0, 2, 1).reshape(PAIRS, P, P).transpose(1, 0, 2)
    shared = _np.concatenate([a["ffn_shared_gate_w"].T, a["ffn_shared_up_w"].T, a["ffn_shared_down_w"].T], axis=1)
    weights = _np.concatenate([shared, _np.concatenate([gu, down], axis=2).reshape(P, PAIRS * W_PAIR)], axis=1)
    arrays = {
        "x_tok": x_tok,
        "small": _np.concatenate([small[name] for name, _ in SMALL], axis=1),
        "weights": weights,
    }
    arrays = {k: _np.ascontiguousarray(v) for k, v in arrays.items()}

    nc = _bacc.Bacc("TRN2", target_bir_lowering=False, num_devices=1)
    aps = [nc.dram_tensor(f"{k}_dram", v.shape, _mybir.dt.from_np(v.dtype), kind="ExternalInput").ap()
           for k, v in arrays.items()]
    out_t = nc.dram_tensor("out_t_dram", (P, T), _mybir.dt.float32, kind="ExternalOutput").ap()
    route_rows = nc.dram_tensor("route_rows_dram", (EXPERTS, T), _mybir.dt.float32, kind="Internal").ap()
    xattn_moe(nc, *aps, route_rows, out_t)
    r = _run(nc, [{f"{k}_dram": v for k, v in arrays.items()}], core_ids=[0])
    return r.results[0]["out_t_dram"].T.reshape(B, SEQ, P)
```
